# Optimizing a Trainium2 kernel written in Bass

```python
import numpy as np
import jax
import jax.numpy as jnp

def _softmax(x, axis=-1):
    return jax.nn.softmax(x, axis=axis)

def _gelu(x):
    return jax.nn.gelu(x, approximate=True)

def _silu(x):
    return jax.nn.silu(x)

def _sigmoid(x):
    return jax.nn.sigmoid(x)

def _layernorm(x, axis=-1, eps=1e-05):
    m = jnp.mean(x, axis=axis, keepdims=True)
    v = jnp.var(x, axis=axis, keepdims=True)
    return (x - m) / jnp.sqrt(v + eps)

def _scatter_add(tgt, idx, src, axis=0):
    return tgt.at[idx].add(src)

def _segment_sum(src, seg, n):
    return jax.ops.segment_sum(src, seg, n)
kernel_name = 'mk_decoder_preln_d1_seqx_r8_860fb2'

def setup_inputs(seed: int=0):
    np.random.seed(seed)
    _w = jnp.asarray

    def _rec_inputs():
        import jax
        import jax.numpy as jnp
        _rk = jax.random.key(seed)
        x = -0.000125 + 0.9999 * jax.random.normal(jax.random.fold_in(_rk, 1), (32, 64, 256), jnp.float32)
        _lenS = 64 - jax.random.randint(jax.random.fold_in(_rk, 7), (32,), 0, max(1, 64 // 4) + 1, jnp.int32)
        _lenS2 = 64 - jax.random.randint(jax.random.fold_in(_rk, 8), (32,), 0, max(1, 64 // 4) + 1, jnp.int32)
        _ctx_2048P = jax.random.normal(jax.random.fold_in(_rk, 11), (32, 16, 256), jnp.float32)
        _ctx_2048c = jax.random.dirichlet(jax.random.fold_in(_rk, 511), 0.3 * jnp.ones((16,), jnp.float32), (32, 64))
        _ctx_2048t = jnp.einsum('bsk,bkd->bsd', _ctx_2048c, _ctx_2048P)
        _ctx_2048t = _ctx_2048t * jax.lax.rsqrt(jnp.mean(jnp.square(_ctx_2048t)) + 1e-12) * 0.953939
        ctx_2048 = -0.000514642 + 1.00011 * (_ctx_2048t + 0.3 * jax.random.normal(jax.random.fold_in(_rk, 611), (32, 64, 256), jnp.float32))
        _validS = jnp.arange(64)[None, :] < _lenS[:, None]
        _validS2 = jnp.arange(64)[None, :] < _lenS2[:, None]
        _causal = jnp.tril(jnp.ones((64, 64), dtype=bool))
        mask_BxS2_bk0 = jnp.logical_not(jnp.broadcast_to(_validS2[:, :], (32, 64)))
        return (x, ctx_2048, mask_BxS2_bk0)
    x, ctx_2048, mask_BxS2_bk0 = _rec_inputs()

    def _L0_attn_setup():
        import jax, jax.numpy as jnp
        import numpy as np
        NUM_HEADS = 16
        key = jax.random.key(seed)
        k1, k2, k3 = jax.random.split(key, 3)
        B, S, H = (2, 256, 256)
        x = jax.random.normal(k1, (B, S, H), dtype=jnp.float32)
        lim_qkv = (6.0 / (H + 3 * H)) ** 0.5
        lim_out = (6.0 / (H + H)) ** 0.5
        Wqkv = jax.random.uniform(k2, (3 * H, H), jnp.float32, -lim_qkv, lim_qkv)
        bqkv = jnp.zeros((3 * H,), jnp.float32)
        Wout = jax.random.uniform(k3, (H, H), jnp.float32, -lim_out, lim_out)
        bout = jnp.zeros((H,), jnp.float32)
        return {'x': x, 'Wqkv': Wqkv, 'bqkv': bqkv, 'Wout': Wout, 'bout': bout}
    _L0_attn_all = _L0_attn_setup()
    _L0_attn_in = {k: v for k, v in _L0_attn_all.items() if k in ('Wqkv', 'bqkv', 'Wout', 'bout')}
    del _L0_attn_all

    def _L0_xattn_setup():
        import jax, jax.numpy as jnp
        import numpy as np
        H = 256
        NH = 16
        HD = H // NH
        EPS = 1e-06

        def rmsnorm(x, w, eps=EPS):
            var = jnp.mean(x * x, axis=-1, keepdims=True)
            return x * jax.lax.rsqrt(var + eps) * w
        key = jax.random.key(seed)
        ks = jax.random.split(key, 9)
        B, L, M = (4, 512, 32)
        s = 1.0 / np.sqrt(H)
        return {'hidden_states': jax.random.normal(ks[0], (B, L, H), dtype=jnp.float32), 'memory_tokens': jax.random.normal(ks[1], (B, M, H), dtype=jnp.float32), 'memory_mask': jax.random.randint(ks[2], (B, M), 0, 2).astype(bool), 'norm_w': jnp.ones((H,), dtype=jnp.float32), 'wq': jax.random.normal(ks[3], (H, H), dtype=jnp.float32) * s, 'wk': jax.random.normal(ks[4], (H, H), dtype=jnp.float32) * s, 'wv': jax.random.normal(ks[5], (H, H), dtype=jnp.float32) * s, 'wo': jax.random.normal(ks[6], (H, H), dtype=jnp.float32) * s, 'wg': jax.random.normal(ks[7], (H, H), dtype=jnp.float32) * s}
    _L0_xattn_all = _L0_xattn_setup()
    _L0_xattn_in = {k: v for k, v in _L0_xattn_all.items() if k in ('norm_w', 'wq', 'wk', 'wv', 'wo', 'wg')}
    del _L0_xattn_all

    def _L0_ffn_setup():
        import jax, jax.numpy as jnp
        import numpy as np
        D_MODEL = 256
        D_FF = 176
        N_EXPERTS = 6
        TOP_K = 2
        B, S = (8, 512)
        key = jax.random.key(seed)
        ks = jax.random.split(key, 6)
        x = jax.random.normal(ks[0], (B, S, D_MODEL), dtype=jnp.float32)
        W1 = jax.random.normal(ks[1], (N_EXPERTS, D_MODEL, D_FF), dtype=jnp.float32) * 0.02
        b1 = jax.random.normal(ks[2], (N_EXPERTS, D_FF), dtype=jnp.float32) * 0.02
        W2 = jax.random.normal(ks[3], (N_EXPERTS, D_FF, D_MODEL), dtype=jnp.float32) * 0.02
        b2 = jax.random.normal(ks[4], (N_EXPERTS, D_MODEL), dtype=jnp.float32) * 0.02
        gate_W = jax.random.normal(ks[5], (N_EXPERTS, D_MODEL), dtype=jnp.float32) * 0.02
        return {'x': x, 'gate_W': gate_W, 'W1': W1, 'b1': b1, 'W2': W2, 'b2': b2}
    _L0_ffn_all = _L0_ffn_setup()
    _L0_ffn_in = {k: v for k, v in _L0_ffn_all.items() if k in ('gate_W', 'W1', 'b1', 'W2', 'b2')}
    del _L0_ffn_all
    return {'x': x, 'ctx_2048': ctx_2048, 'mask_BxS2_bk0': mask_BxS2_bk0, 'L0_attn_Wqkv': _L0_attn_in['Wqkv'], 'L0_attn_bqkv': _L0_attn_in['bqkv'], 'L0_attn_Wout': _L0_attn_in['Wout'], 'L0_attn_bout': _L0_attn_in['bout'], 'L0_xattn_norm_w': _L0_xattn_in['norm_w'], 'L0_xattn_wq': _L0_xattn_in['wq'], 'L0_xattn_wk': _L0_xattn_in['wk'], 'L0_xattn_wv': _L0_xattn_in['wv'], 'L0_xattn_wo': _L0_xattn_in['wo'], 'L0_xattn_wg': _L0_xattn_in['wg'], 'L0_ffn_gate_W': _L0_ffn_in['gate_W'], 'L0_ffn_W1': _L0_ffn_in['W1'], 'L0_ffn_b1': _L0_ffn_in['b1'], 'L0_ffn_W2': _L0_ffn_in['W2'], 'L0_ffn_b2': _L0_ffn_in['b2']}

def reference(x, ctx_2048, mask_BxS2_bk0, L0_attn_Wqkv, L0_attn_bqkv, L0_attn_Wout, L0_attn_bout, L0_xattn_norm_w, L0_xattn_wq, L0_xattn_wk, L0_xattn_wv, L0_xattn_wo, L0_xattn_wg, L0_ffn_gate_W, L0_ffn_W1, L0_ffn_b1, L0_ffn_W2, L0_ffn_b2):
    import jax
    import jax.numpy as jnp

    def _L0_attn_ref(x, Wqkv, bqkv, Wout, bout):
        import jax, jax.numpy as jnp
        import numpy as np
        NUM_HEADS = 16
        B, S, H = x.shape
        nh = NUM_HEADS
        hd = H // nh
        qkv = jnp.einsum('bsh,oh->bso', x, Wqkv) + bqkv
        q, k, v = jnp.split(qkv, 3, axis=-1)
        q = q.reshape(B, S, nh, hd).transpose(0, 2, 1, 3)
        k = k.reshape(B, S, nh, hd).transpose(0, 2, 1, 3)
        v = v.reshape(B, S, nh, hd).transpose(0, 2, 1, 3)
        scale = hd ** (-0.5)
        scores = jnp.einsum('bhqd,bhkd->bhqk', q, k) * scale
        causal = jnp.triu(jnp.ones((S, S), dtype=bool), k=1)
        scores = jnp.where(causal, -jnp.inf, scores)
        attn = jax.nn.softmax(scores, axis=-1)
        out = jnp.einsum('bhqk,bhkd->bhqd', attn, v)
        out = out.transpose(0, 2, 1, 3).reshape(B, S, H)
        return jnp.einsum('bsh,oh->bso', out, Wout) + bout

    def _L0_xattn_ref(hidden_states, memory_tokens, memory_mask, norm_w, wq, wk, wv, wo, wg):
        import jax, jax.numpy as jnp
        import numpy as np
        H = 256
        NH = 16
        HD = H // NH
        EPS = 1e-06

        def rmsnorm(x, w, eps=EPS):
            var = jnp.mean(x * x, axis=-1, keepdims=True)
            return x * jax.lax.rsqrt(var + eps) * w
        B, L, C = hidden_states.shape
        M = memory_tokens.shape[1]
        scale = HD ** (-0.5)
        x = rmsnorm(hidden_states, norm_w)
        q = (x @ wq.T).reshape(B, L, NH, HD)
        k = (memory_tokens @ wk.T).reshape(B, M, NH, HD)
        v = (memory_tokens @ wv.T).reshape(B, M, NH, HD)
        attn = jnp.einsum('blhd,bmhd->bhlm', q, k) * scale
        attn = jnp.where(memory_mask[:, None, None, :], attn, -jnp.inf)
        attn = jax.nn.softmax(attn, axis=-1)
        attn = jnp.nan_to_num(attn, nan=0.0)
        out = jnp.einsum('bhlm,bmhd->blhd', attn, v).reshape(B, L, C)
        out = out @ wo.T
        gate = jax.nn.sigmoid(x @ wg.T)
        return gate * out

    def _L0_ffn_ref(x, gate_W, W1, b1, W2, b2):
        import jax, jax.numpy as jnp
        import numpy as np
        D_MODEL = 256
        D_FF = 176
        N_EXPERTS = 6
        TOP_K = 2
        B, S = (8, 512)
        gate_logits = jnp.einsum('bd,ed->be', x.mean(axis=1), gate_W)
        gate_probs = jax.nn.softmax(gate_logits, axis=-1)
        topk_vals, topk_idx = jax.lax.top_k(gate_probs, TOP_K)
        topk_vals = topk_vals / topk_vals.sum(axis=-1, keepdims=True)
        W1g = W1[topk_idx]
        b1g = b1[topk_idx]
        W2g = W2[topk_idx]
        b2g = b2[topk_idx]
        h = jnp.einsum('bsd,bkdf->bksf', x, W1g) + b1g[:, :, None, :]
        h = jax.nn.gelu(h, approximate=False)
        eo = jnp.einsum('bksf,bkfd->bksd', h, W2g) + b2g[:, :, None, :]
        return jnp.einsum('bk,bksd->bsd', topk_vals, eo)
    x = x + _L0_attn_ref(_layernorm(x, axis=-1), L0_attn_Wqkv, L0_attn_bqkv, L0_attn_Wout, L0_attn_bout)
    x = x + _L0_xattn_ref(_layernorm(x, axis=-1), ctx_2048, mask_BxS2_bk0, L0_xattn_norm_w, L0_xattn_wq, L0_xattn_wk, L0_xattn_wv, L0_xattn_wo, L0_xattn_wg)
    x = x + _L0_ffn_ref(_layernorm(x, axis=-1), L0_ffn_gate_W, L0_ffn_W1, L0_ffn_b1, L0_ffn_W2, L0_ffn_b2)
    return x

_drawn_inputs = setup_inputs


def setup_inputs(seed=0):
    import zlib

    import numpy as np

    out = dict(_drawn_inputs(seed))
    spreads = {'L0_attn_bqkv': (0.0, 0.1), 'L0_attn_bout': (0.0, 0.1), 'L0_xattn_norm_w': (1.0, 0.2)}
    factors = {'L0_ffn_b1': 28.432, 'L0_ffn_b2': 4.395}
    for name, (base, spread) in spreads.items():
        noise = np.random.default_rng([zlib.crc32(name.encode()), seed]).standard_normal(out[name].shape)
        drawn = base * np.exp(spread * noise) if base else spread * noise
        out[name] = jnp.asarray(drawn.astype(out[name].dtype))
    for name, factor in factors.items():
        out[name] = (out[name] * factor).astype(out[name].dtype)
    return out
```

```python
from contextlib import ExitStack

import numpy as np

import concourse.bass as bass
from concourse import mybir

ALU = mybir.AluOpType
ACT = mybir.ActivationFunctionType
AX = mybir.AxisListType
F32 = mybir.dt.float32
U32 = mybir.dt.uint32
U8 = mybir.dt.uint8

B, S, H = 32, 64, 256
NH, HD = 16, 16
E, F, TOPK = 6, 176, 2
P = 128
KC = H // P
BT = P // S
T = B // BT
HP = NH // 2
HQ = P // (2 * HD)
FH = F // 2
VW = HD + 1
SELF, CROSS = 0, 1
HIDDEN = -1e30
FLOOR = -1e29
LN_EPS, RMS_EPS = 1e-5, 1e-6

C_IDENT = 0
C_CAUSAL = C_IDENT + P
C_HEADS = C_CAUSAL + S
C_IOTA = C_HEADS + 2 * S
C_TILE = C_IOTA + E
C_SPREAD = C_TILE + T
C_END = C_SPREAD + P


def shape_constants():
    c = np.zeros((P, C_END), np.float32)
    p = np.arange(P)
    c[:, C_IDENT:C_IDENT + P] = np.eye(P)
    c[:, C_CAUSAL:C_CAUSAL + S] = np.where(np.arange(S)[None] > (p % S)[:, None], HIDDEN, 0.0)
    for odd in range(2):
        c[:, C_HEADS + odd * S:C_HEADS + (odd + 1) * S] = ((p // HD % 2 == odd) * HD ** -0.5)[:, None]
    c[:, C_IOTA:C_IOTA + E] = np.arange(E)
    c[:B, C_TILE:C_TILE + T] = (p[:B, None] // BT == np.arange(T)[None])
    c[:B, C_SPREAD:C_SPREAD + P] = (p[:B, None] % BT == (p // S)[None])
    return c


def decoder_layer(nc, x, ctxT, hidden, consts, wqkvT, bqkv, woutT, bout, norm_w, wqT, wkT, wvT, woT, wgT,
                  gateT, w1, b1, w2, b2, out):
    ctx = ExitStack()
    with ctx:
        def sb(name, shape, dt=F32):
            return ctx.enter_context(nc.sbuf_tensor(name, shape, dt))

        def sem(name):
            return ctx.enter_context(nc.semaphore(name))

        bank = [ctx.enter_context(nc.psum_tensor(f"bank{i}", [P, 512], F32)) for i in range(8)]

        X = sb("X", [P, T, H])
        const = sb("const", [P, C_END])
        ident = const[:, C_IDENT:C_IDENT + P]
        causal = const[:, C_CAUSAL:C_CAUSAL + S]
        heads = const[:, C_HEADS:C_HEADS + 2 * S].rearrange("p (h q) -> p h q", h=2)
        ones = sb("ones", [P, P])
        minus_half = sb("minus_half", [P, 1])
        ln_eps = sb("ln_eps", [P, 1])
        rms_eps = sb("rms_eps", [P, 1])
        mf = [None] + [sb(f"mf{l}", [P, T, 2]) for l in (1, 2)]

        wqkv_sb = sb("wqkv_sb", [P, KC, 3 * H])
        bqk = sb("bqk", [P, 2 * KC])
        bv = sb("bv", [P, 2])
        bout_row = sb("bout_row", [1, H])
        wo_sb = [sb("wout_sb", [P, 2, H]), sb("wo_sb", [P, 2, H])]
        nw = sb("nw", [P, KC])
        wx = {n: sb(f"w{n}_sb", [P, KC, H]) for n in "qkvg"}
        bvb = sb("bvb", [P, 2, P])
        bias_rows = sb("bias_rows", [P, H])
        cT = [sb(f"cT{i}", [P, KC, P]) for i in range(2)]
        hid8 = sb("hid8", [P, B * S], U8)
        hide = sb("hide", [P, B * S])

        six0 = sb("six0", [P, 6])
        mv0 = sb("mv0", [P, 4])
        six1 = sb("six1", [P, 6])
        mv1 = sb("mv1", [P, 4])
        xn = sb("xn", [P, H])
        xnT = sb("xnT", [P, KC, P])
        qm = sb("qm", [P, KC, BT, 2, S])
        kT = sb("kT", [P, KC, P])
        kd = sb("kd", [P, KC, HQ, P])
        vd = [sb(f"vd{i}", [P, NH, BT, VW]) for i in range(2)]
        th = [sb(f"th{i}", [P, H]) for i in range(2)]
        sm = [sb(f"sm{c}", [P, HQ, BT, S]) for c in range(KC)]
        mx = [sb(f"mx{c}", [P, BT * HQ]) for c in range(KC)]
        pr = [sb(f"pr{c}", [P, HQ, BT, S]) for c in range(KC)]
        pT = [sb(f"pT{c}", [P, HQ, P]) for c in range(KC)]
        rsum = sb("rsum", [P, HP, BT])
        rinv = sb("rinv", [P, HP, BT])
        on = sb("on", [P, BT, HP, HD])
        oT = sb("oT", [P, 2, BT, S])
        gated = sb("gated", [P, H])

        w1_sb = sb("w1_sb", [P, E, KC, F])
        w2_sb = sb("w2_sb", [FH + 1, E, 2, H])
        b1_sb = sb("b1_sb", [E, F])
        gw_sb = sb("gw_sb", [P, KC, E])
        zT = sb("zT", [P, KC, B * S])
        zsum = sb("zsum", [P, KC, B])
        w1c = [sb(f"w1c{i}", [P, BT, TOPK, KC, F]) for i in range(2)]
        w2c = [sb(f"w2c{i}", [FH + 1, BT, TOPK, 2, H]) for i in range(2)]
        logit = sb("logit", [B, 8])
        top = sb("top", [B, 8])
        ntop = sb("ntop", [B, 1])
        ex = sb("ex", [B, E])
        exs = sb("exs", [B, 2])
        prob = sb("prob", [B, 8])
        p8 = sb("p8", [B, 8])
        i8 = sb("i8", [B, 8], U32)
        i8f = sb("i8f", [B, TOPK])
        cs = sb("cs", [B, 2])
        cw = sb("cw", [B, TOPK])
        pick = sb("pick", [B, TOPK, E])
        pickT = sb("pickT", [E, TOPK, B])
        ctile = sb("ctile", [B, T, TOPK])
        ctok = sb("ctok", [P, T, TOPK])
        irow = sb("irow", [1, B * TOPK], U32)
        b1s = sb("b1s", [FH, B, TOPK, 2])
        hb = sb("hb", [FH, BT * TOPK * 2, S])
        hT = sb("hT", [P, BT * TOPK * 2, S])
        part = sb("part", [P, H])
        res = [sb(f"res{i}", [P, H]) for i in range(2)]

        x_in0, x_in1, c_in, w_in, cross_in, ffn_in = (
            sem(n) for n in ("x_in0", "x_in1", "c_in", "w_in", "cross_in", "ffn_in"))
        ctx_in = [sem(f"ctx_in{i}") for i in range(2)]
        setup_pool, setup_dve, bias_mm, bias_b, bias_ready = (
            sem(n) for n in ("setup_pool", "setup_dve", "bias_mm", "bias_b", "bias_ready"))
        six0_ready, mv0_ready, factor0 = sem("six0_ready"), sem("mv0_ready"), sem("factor0")
        six1_ready, mv1_ready = sem("six1_ready"), sem("mv1_ready")
        factor1 = [sem(f"factor1_{l}") for l in range(2)]
        mf_ready = [None] + [sem(f"mf_ready{l}") for l in (1, 2)]
        xn_ready, xb_ready = sem("xn_ready"), sem("xb_ready")
        x_done, xT_ready = sem("x_done"), sem("xT_ready")
        q_done, k_done, v_done, g_done = (sem(n) for n in ("q_done", "k_done", "v_done", "g_done"))
        q_ready, k_ready, kd_ready, v_ready, th_ready = (
            sem(n) for n in ("q_ready", "k_ready", "kd_ready", "v_ready", "th_ready"))
        s_done = [sem(f"s_done{c}") for c in range(KC)]
        masked = [sem(f"masked{c}") for c in range(KC)]
        mx_ready = [sem(f"mx_ready{c}") for c in range(KC)]
        mx_kept = [sem(f"mx_kept{c}") for c in range(KC)]
        less = [sem(f"less{c}") for c in range(KC)]
        pr_ready = [sem(f"pr_ready{c}") for c in range(KC)]
        t_done = [sem(f"t_done{c}") for c in range(KC)]
        pT_ready = [sem(f"pT_ready{c}") for c in range(KC)]
        pv_done, sum_kept, sum_inv, on_ready = (sem(n) for n in ("pv_done", "sum_kept", "sum_inv", "on_ready"))
        o_done, oT_ready, wo_done, gate_done, x_ready = (
            sem(n) for n in ("o_done", "oT_ready", "wo_done", "gate_done", "x_ready"))
        z_ready, zt_done, zT_ready, zs_ready = (sem(n) for n in ("z_ready", "zt_done", "zT_ready", "zs_ready"))
        gate_dve, gate_pe, gate_act, irow_in = (sem(n) for n in ("gate_dve", "gate_pe", "gate_act", "irow_in"))
        w_copied = [sem(f"w_copied{i}") for i in range(2)]
        h_done, hb_ready, hT_ready, y_done, part_ready, res_ready = (
            sem(n) for n in ("h_done", "hb_ready", "hT_ready", "y_done", "part_ready", "res_ready"))
        stored = [sem(f"stored{i}") for i in range(2)]

        N_CONST, N_W, N_CTX, N_FFN = 1, 14, 2, 6

        def reached(eng, s, n):
            if not isinstance(n, int) or n > 0:
                eng.wait_ge(s, n)

        def alone(eng, s):
            eng.wait_ge(s, 1)

        def held(eng, n):
            return n if isinstance(n, int) else eng.snap(eng.to_reg(n))

        def tile_of(buf, t):
            return buf[:, bass.ds(t, 1), :].rearrange("p a h -> p (a h)")

        def attention_steps(eng, step):
            step(-1, 1, SELF, None, None, None)
            step(0, 0, SELF, SELF, None, None)
            step(1, 1, SELF, SELF, SELF, None)
            step(2, 0, SELF, SELF, SELF, SELF)
            with eng.Fori(3, T - 2, 2) as j:
                step(j, 1, SELF, SELF, SELF, SELF)
                step(j + 1, 0, SELF, SELF, SELF, SELF)
            step(T - 1, 1, CROSS, SELF, SELF, SELF)
            step(T, 0, CROSS, CROSS, SELF, SELF)
            step(T + 1, 1, CROSS, CROSS, CROSS, SELF)
            step(T + 2, 0, CROSS, CROSS, CROSS, CROSS)
            with eng.Fori(T + 3, 2 * T - 2, 2) as j:
                step(j, 1, CROSS, CROSS, CROSS, CROSS)
                step(j + 1, 0, CROSS, CROSS, CROSS, CROSS)
            step(2 * T - 1, 1, None, CROSS, CROSS, CROSS)
            step(2 * T, 0, None, None, CROSS, CROSS)
            step(2 * T + 1, 1, None, None, None, CROSS)

        def expert_steps(eng, step):
            step(0, 0, True, False, False)
            step(1, 1, True, True, False)
            step(2, 0, True, True, True)
            step(3, 1, True, True, True)
            with eng.Fori(4, T - 1, 2) as j:
                step(j, 0, True, True, True)
                step(j + 1, 1, True, True, True)
            step(T, 0, False, True, True)
            step(T + 1, 1, False, False, True)

        block = ctx.enter_context(nc.Block())

        @block.sync
        def _(sp):
            xt = x.rearrange("(t p) h -> p t h", p=P)
            sp.dma_start(X[:, 0:2, :], xt[:, 0:2, :]).then_inc(x_in0, 16)
            sp.dma_start(const[:], consts).then_inc(c_in, 16)
            sp.dma_start(wqkv_sb[:], wqkvT.rearrange("(c p) o -> p c o", p=P)).then_inc(w_in, 16)
            sp.dma_start(X[:, 2:T, :], xt[:, 2:T, :]).then_inc(x_in1, 16)
            with nc.allow_non_contiguous_dma("a few biases, down the partitions"):
                sp.dma_start(bqk[:], bqkv[0:2 * H].rearrange("(c p) -> p c", p=P)).then_inc(w_in, 16)
                for r in range(HP):
                    sp.dma_start(bv[r * HD:(r + 1) * HD, :],
                                 bqkv[2 * H + 2 * r * HD:2 * H + 2 * (r + 1) * HD].rearrange("(h d) -> d h", d=HD)
                                 ).then_inc(w_in, 16)
                sp.dma_start(nw[:], norm_w.rearrange("(c p) -> p c", p=P)).then_inc(w_in, 16)
            sp.dma_start(bout_row[:], bout.rearrange("(a h) -> a h", a=1)).then_inc(w_in, 16)
            sp.dma_start(wo_sb[SELF][:], woutT).then_inc(w_in, 16)
            sp.dma_start(wo_sb[CROSS][:], woT).then_inc(w_in, 16)

            def step(j, i, ln, la, lb, lc):
                if la == CROSS:
                    if not isinstance(j, int) or j > T + 1:
                        sp.wait_ge(v_done, j - 1)
                    sp.dma_start(cT[i][:], ctxT.rearrange("(c p) n -> p c n", p=P)[:, :, bass.ds((j - T) * P, P)]
                                 ).then_inc(ctx_in[i], 16)
                if la is not None:
                    sp.wait_ge(k_ready, j + 1)
                    reached(sp, s_done[1], j)
                    for r in range(HQ):
                        rows = slice(r * 2 * HD, (r + 1) * 2 * HD)
                        sp.dma_start(kd[rows, :, r, :], kT[rows, :, :]).then_inc(kd_ready, 16)
                if isinstance(j, int) and j == T:
                    sp.dma_start(w1_sb[:], w1.rearrange("e (c p) f -> p e c f", p=P)).then_inc(ffn_in, 16)
                    sp.dma_start(w2_sb[0:FH, :, :, :], w2.rearrange("e (a p) h -> p e a h", p=FH)).then_inc(ffn_in, 16)
                    for a in range(2):
                        sp.dma_start(w2_sb[FH:FH + 1, :, a, :], b2.rearrange("(q e) h -> q e h", q=1)).then_inc(ffn_in, 16)
                    sp.dma_start(b1_sb[:], b1).then_inc(ffn_in, 16)
                    sp.dma_start(gw_sb[:], gateT.rearrange("(c p) e -> p c e", p=P)).then_inc(ffn_in, 16)

            attention_steps(sp, step)

            sp.wait_ge(gate_dve, 7)
            sp.dma_start(irow[:], i8[:, 0:TOPK]).then_inc(irow_in, 16)
            sp.wait_ge(irow_in, 16)
            sp.wait_ge(ffn_in, 16 * N_FFN)

            def expert_step(j, i, load, up, down):
                if load:
                    reached(sp, h_done, j - 1)
                    reached(sp, y_done, j - 1)
                    for b in range(BT):
                        for k in range(TOPK):
                            e = sp.value_load(irow[0:1, bass.ds(j * (BT * TOPK) + (b * TOPK + k), 1)], min_val=0, max_val=E - 1)
                            sp.dma_start(w1c[i][:, b, k, :, :], w1_sb[:, bass.ds(e, 1), :, :].rearrange("p a c f -> p (a c) f")
                                         ).then_inc(w_copied[i], 16)
                            sp.dma_start(w2c[i][:, b, k, :, :], w2_sb[:, bass.ds(e, 1), :, :].rearrange("p a c f -> p (a c) f")
                                         ).then_inc(w_copied[i], 16)
                if down:
                    sp.wait_ge(res_ready, j - 1)
                    sp.dma_start(out[bass.ds((j - 2) * P, P), :], res[i][:]).then_inc(stored[i], 16)

            expert_steps(sp, expert_step)
            for i in range(2):
                sp.wait_ge(stored[i], 16 * (T // 2))

        @block.gpsimd
        def _(pool):
            pool.memset(minus_half[:], -0.5).then_inc(setup_pool, 1)
            pool.memset(kd[:], 0.0).then_inc(setup_pool, 1)
            for i in range(2):
                pool.memset(vd[i][:], 0.0).then_inc(setup_pool, 1)
            pool.memset(ln_eps[:], LN_EPS).then_inc(setup_pool, 1)
            pool.memset(rms_eps[:], RMS_EPS).then_inc(setup_pool, 1)
            pool.wait_ge(setup_pool, 6)
            for i in range(2):
                for b in range(BT):
                    pool.memset(vd[i][b * S:(b + 1) * S, :, b, HD:VW], 1.0).then_inc(setup_pool, 1)
            pool.wait_ge(setup_pool, 10)

            def step(j, i, ln, la, lb, lc):
                if ln == SELF:
                    n = j + 1
                    pool.wait_ge(mv0_ready, n + 1)
                    pool.tensor_tensor(mv0[:, 3:4], mv0[:, 1:2], ln_eps[:], ALU.add).then_inc(factor0, 1)
                    pool.wait_ge(factor0, 2 * n + 1)
                    pool.tensor_tensor(mv0[:, 2:3], mv0[:, 3:4], minus_half[:], ALU.pow).then_inc(factor0, 1)
                if lb is not None:
                    t = j - 1
                    for c in range(KC):
                        maxima = held(pool, t + 1)
                        if lb == CROSS:
                            alone(pool, setup_pool)
                        pool.wait_ge(mx_ready[c], maxima)
                        if lb == CROSS:
                            pool.tensor_scalar(mx[c][:], mx[c][:], FLOOR, None, ALU.max).then_inc(mx_kept[c], 1)
                            pool.wait_ge(mx_kept[c], t - T + 1)
                        s3 = sm[c][:].rearrange("p h b k -> p (h b) k")
                        pool.tensor_tensor(s3, s3, mx[c][:].unsqueeze(2).to_broadcast([P, BT * HQ, S]), ALU.subtract
                                           ).then_inc(less[c], 1)
                if lc is not None:
                    t = j - 2
                    u = t - lc * T
                    chain, a, r, f = factor1[lc], mv1[:, 3:4], mv1[:, 1:2], mv1[:, 2:3]
                    per = 7 if lc == SELF else 2
                    pool.wait_ge(mv1_ready, t + 1)
                    pool.tensor_tensor(a, r, ln_eps[:], ALU.add).then_inc(chain, 1)
                    pool.wait_ge(chain, per * u + 1)
                    pool.tensor_tensor(f, a, minus_half[:], ALU.pow).then_inc(chain, 1)
                    if lc == SELF:
                        pool.wait_ge(chain, per * u + 2)
                        pool.tensor_tensor(a, r, f, ALU.mult).then_inc(chain, 1)
                        pool.wait_ge(chain, per * u + 3)
                        pool.tensor_tensor(a, a, f, ALU.mult).then_inc(chain, 1)
                        pool.wait_ge(chain, per * u + 4)
                        pool.tensor_tensor(a, a, rms_eps[:], ALU.add).then_inc(chain, 1)
                        pool.wait_ge(chain, per * u + 5)
                        pool.tensor_tensor(a, a, minus_half[:], ALU.pow).then_inc(chain, 1)
                        pool.wait_ge(chain, per * u + 6)
                        pool.tensor_tensor(f, f, a, ALU.mult).then_inc(chain, 1)
                    alone(pool, setup_pool)
                    pool.wait_ge(chain, per * u + per)
                    pool.tensor_copy(tile_of(mf[lc + 1], u), mv1[:, 0:3:2]).then_inc(mf_ready[lc + 1], 1)
                if ln == SELF:
                    n = j + 1
                    alone(pool, setup_pool)
                    if isinstance(j, int) and j == -1:
                        pool.wait_ge(bias_ready, 1)
                    pool.wait_ge(xn_ready, n + 1)
                    pool.tensor_tensor(tile_of(X, n), tile_of(X, n), bias_rows[:], ALU.add).then_inc(xb_ready, 1)

            attention_steps(pool, step)

        @block.scalar
        def _(act):
            act.dma_start(hid8[:], hidden.rearrange("(a n) -> a n", a=1).to_broadcast([P, B * S])).then_inc(cross_in, 16)
            for n in "qkvg":
                act.dma_start(wx[n][:], {"q": wqT, "k": wkT, "v": wvT, "g": wgT}[n].rearrange("(c p) o -> p c o", p=P)
                              ).then_inc(w_in, 16) if n in "qg" else \
                    act.dma_start(wx[n][:], {"k": wkT, "v": wvT}[n].rearrange("(c p) o -> p c o", p=P)).then_inc(cross_in, 16)
            act.wait_ge(bias_mm, 1)
            act.copy(bias_rows[:], bank[3][:, 0:H]).then_inc(bias_ready, 1)

            def step(j, i, ln, la, lb, lc):
                if lc is not None:
                    t = j - 2
                    for c in range(KC):
                        act.wait_ge(t_done[c], t + 1)
                        reached(act, pv_done, t)
                        act.copy(pT[c][:].rearrange("p h q -> p (h q)"), bank[c][:]).then_inc(pT_ready[c], 1)
                if la is not None:
                    act.wait_ge(x_done, j + 1)
                    reached(act, v_done, j)
                    if la == CROSS:
                        reached(act, g_done, j - T)
                    act.copy(xnT[:].rearrange("p c t -> p (c t)"), bank[2][:, 0:H]).then_inc(xT_ready, 1)
                if lc is not None:
                    act.wait_ge(o_done, t + 1)
                    reached(act, wo_done, t)
                    act.copy(oT[:].rearrange("p h b q -> p b h q"), bank[2][:, 0:H].rearrange("p (b h q) -> p b h q", b=BT, h=2)).then_inc(oT_ready, 1)

                def softmax(c):
                    t = j - 1
                    act.wait_ge(less[c], t + 1)
                    reached(act, t_done[c], t)
                    act.activation(pr[c][:].rearrange("p h b k -> p (h b k)"), sm[c][:].rearrange("p h b k -> p (h b k)"),
                                   ACT.Exp).then_inc(pr_ready[c], 1)

                if lb is not None:
                    softmax(0)
                if la is not None:
                    act.wait_ge(k_done, j + 1)
                    reached(act, kd_ready, 16 * HQ * j)
                    if la == SELF:
                        for c in range(KC):
                            ins = act.activation(kT[:, c, :], bank[7][:, c * P:(c + 1) * P], ACT.Identity, bias=bqk[:, KC + c:KC + c + 1])
                    else:
                        ins = act.copy(kT[:].rearrange("p c t -> p (c t)"), bank[7][:, 0:H])
                    ins.then_inc(k_ready, 1)
                if lb is not None:
                    softmax(1)
                if la is not None:
                    act.wait_ge(v_done, j + 1)
                    reached(act, pv_done, j - 1)
                    for b in range(BT):
                        rows = slice(b * S, (b + 1) * S)
                        ins = act.copy(vd[i][rows, :, b, 0:HD], bank[7][rows, H:2 * H].rearrange("p (h d) -> p h d", d=HD))
                    ins.then_inc(v_ready, 1)
                if la == CROSS:
                    act.wait_ge(g_done, j - T + 1)
                    reached(act, gate_done, j - T - 1)
                    act.activation(th[i][:], bank[6][:, H:2 * H], ACT.Tanh, scale=0.5).then_inc(th_ready, 1)

            attention_steps(act, step)

            def norm_step(t):
                alone(act, setup_dve)
                act.wait_ge(zt_done, t + 1)
                act.copy(zT[:, :, bass.ds(t * P, P)], bank[2][:, 0:H].rearrange("p (c t) -> p c t", c=KC)).then_inc(zT_ready, 1)

            with act.Fori(0, T) as t:
                norm_step(t)

            act.wait_ge(gate_dve, 3)
            act.activation(ex[:], logit[:, 0:E], ACT.Exp, bias=ntop[:, 0:1], accum_out=exs[:, 0:1]).then_inc(gate_act, 1)

            def expert_step(j, i, load, up, down):
                if up:
                    t = j - 1
                    act.wait_ge(hb_ready, t + 1)
                    reached(act, y_done, t)
                    act.activation(hT[0:FH, :, :].rearrange("p n t -> p (n t)"), hb[:].rearrange("p n t -> p (n t)"), ACT.Gelu
                                   ).then_inc(hT_ready, 1)

            expert_steps(act, expert_step)

        @block.vector
        def _(dve):
            dve.memset(ones[:], 1.0).then_inc(setup_dve, 1)
            dve.memset(hT[:], 1.0).then_inc(setup_dve, 1)
            dve.memset(logit[:], HIDDEN).then_inc(setup_dve, 1)
            dve.memset(prob[:], -1.0).then_inc(setup_dve, 1)
            dve.wait_ge(w_in, 16 * (N_W + 2))
            dve.wait_ge(setup_dve, 4)
            for h in range(2):
                ins = dve.tensor_scalar(bvb[:, h, :], ones[:], bv[:, h:h + 1], None, ALU.mult)
            ins.then_inc(bias_b, 1)
            for n in "qg":
                for c in range(KC):
                    ins = dve.tensor_scalar(wx[n][:, c, :], wx[n][:, c, :], nw[:, c:c + 1], None, ALU.mult)
            ins.then_inc(bias_b, 1)
            dve.wait_ge(c_in, 16)

            def step(j, i, ln, la, lb, lc):
                if ln == SELF:
                    n = j + 1
                    alone(dve, setup_dve)
                    if isinstance(j, int) and j < 2:
                        dve.wait_ge(*((x_in1, 16) if n > 1 else (x_in0, 16)))
                    reached(dve, mv0_ready, n)
                    dve.bn_stats(six0[:], tile_of(X, n)).then_inc(six0_ready, 1)
                    n1 = held(dve, n + 1)
                    alone(dve, setup_dve)
                    dve.wait_ge(six0_ready, n1)
                    reached(dve, xn_ready, n)
                    dve.bn_aggr(mv0[:, 0:2], six0[:]).then_inc(mv0_ready, 1)
                if isinstance(j, int) and j == T:
                    dve.wait_ge(cross_in, 16 * 3)
                    dve.tensor_scalar(hide[:], hid8[:], -1.0, -HIDDEN, ALU.add, ALU.mult).then_inc(setup_dve, 1)
                    dve.wait_ge(setup_dve, 5)
                if lc is not None:
                    t = j - 2
                    O = bank[3][:, 0:HP * BT * VW].rearrange("p (h b d) -> p h b d", h=HP, b=BT)
                    dve.wait_ge(pv_done, t + 1)
                    reached(dve, on_ready, t)
                    if lc == SELF:
                        dve.tensor_scalar(rsum[:], O[:, :, :, HD], 1.0, None, ALU.mult).then_inc(sum_kept, 1)
                    else:
                        dve.tensor_scalar(rsum[:], O[:, :, :, HD], 1e-30, 2.0, ALU.max, ALU.mult).then_inc(sum_kept, 1)
                    dve.wait_ge(sum_kept, t + 1)
                    dve.reciprocal(rinv[:], rsum[:]).then_inc(sum_inv, 1)
                    dve.wait_ge(sum_inv, t + 1)
                    reached(dve, o_done, t)
                    dve.tensor_tensor(on[:].rearrange("p b h d -> p h b d"), O[:, :, :, 0:HD],
                                      rinv[:].unsqueeze(3).to_broadcast([P, HP, BT, HD]), ALU.mult).then_inc(on_ready, 1)
                if lb is not None:
                    t = j - 1
                    for c in range(KC):
                        scores = bank[4 + c][:].rearrange("p (b h k) -> p b h k", b=BT, h=HQ)
                        dve.wait_ge(s_done[c], t + 1)
                        reached(dve, pr_ready[c], t)
                        if lb == SELF:
                            m = causal.unsqueeze(1).to_broadcast([P, BT, S])
                        else:
                            m = hide[:, bass.ds((t - T) * P, P)].rearrange("p (b k) -> p b k", b=BT)
                        dve.tensor_tensor(sm[c][:].rearrange("p h b k -> p b h k"), scores,
                                          m.unsqueeze(2).to_broadcast([P, BT, HQ, S]), ALU.add).then_inc(masked[c], 1)
                        dve.wait_ge(masked[c], t + 1)
                        dve.tensor_reduce(mx[c][:], sm[c][:].rearrange("p h b k -> p (h b) k"), AX.X, ALU.max
                                          ).then_inc(mx_ready[c], 1)
                if la is not None:
                    dve.wait_ge(q_done, j + 1)
                    reached(dve, s_done[1], j)
                    if la == SELF:
                        for c in range(KC):
                            for b in range(BT):
                                qc = bank[6][:, c * P + b * S:c * P + (b + 1) * S].unsqueeze(1).to_broadcast([P, 2, S])
                                ins = dve.scalar_tensor_tensor(out=qm[:, c, b, :, :], in0=qc, scalar=bqk[:, c:c + 1],
                                                               in1=heads, op0=ALU.add, op1=ALU.mult)
                    else:
                        qc = bank[6][:, 0:H].rearrange("p (n q) -> p n q", q=S)
                        ins = dve.tensor_tensor(qm[:].rearrange("p c b h q -> p (c b) h q"),
                                                qc.unsqueeze(2).to_broadcast([P, KC * BT, 2, S]),
                                                heads.unsqueeze(1).to_broadcast([P, KC * BT, 2, S]), ALU.mult)
                    ins.then_inc(q_ready, 1)
                if lc is not None:
                    t = j - 2
                    xt = tile_of(X, t - lc * T)
                    wo = bank[3][:, 0:H]
                    dve.wait_ge(wo_done, t + 1)
                    if lc == SELF:
                        dve.wait_ge(xb_ready, t + 1)
                        dve.tensor_tensor(xt, wo, xt, ALU.add).then_inc(x_ready, 1)
                    else:
                        dve.wait_ge(th_ready, t - T + 1)
                        dve.scalar_tensor_tensor(out=gated[:], in0=th[i][:], scalar=1.0, in1=wo, op0=ALU.add, op1=ALU.mult
                                                 ).then_inc(gate_done, 1)
                        dve.wait_ge(gate_done, t - T + 1)
                        dve.tensor_tensor(xt, gated[:], xt, ALU.add).then_inc(x_ready, 1)
                    alone(dve, setup_dve)
                    dve.wait_ge(x_ready, t + 1)
                    dve.bn_stats(six1[:], xt).then_inc(six1_ready, 1)
                    if lc == SELF:
                        alone(dve, setup_dve)
                        reached(dve, mf_ready[1], t)
                    else:
                        dve.wait_ge(mf_ready[1], T)
                        reached(dve, mf_ready[2], t - T)
                    dve.wait_ge(six1_ready, t + 1)
                    dve.bn_aggr(mv1[:, 0:2], six1[:]).then_inc(mv1_ready, 1)
                if ln is not None:
                    n = j + 1
                    reached(dve, x_done, n)
                    if ln == SELF:
                        dve.wait_ge(factor0, 2 * n + 2)
                        mean, factor = mv0[:, 0:1], mv0[:, 2:3]
                    else:
                        dve.wait_ge(mf_ready[1], n - T + 1)
                        mean, factor = tile_of(mf[1], n - T)[:, 0:1], tile_of(mf[1], n - T)[:, 1:2]
                    dve.tensor_scalar(xn[:], tile_of(X, n - ln * T), mean, factor, ALU.subtract, ALU.mult).then_inc(xn_ready, 1)

            attention_steps(dve, step)

            def norm_step(t):
                dve.wait_ge(mf_ready[2], t + 1)
                reached(dve, zt_done, t)
                m = tile_of(mf[2], t)
                dve.tensor_scalar(xn[:], tile_of(X, t), m[:, 0:1], m[:, 1:2], ALU.subtract, ALU.mult).then_inc(z_ready, 1)
                alone(dve, setup_dve)
                dve.wait_ge(zT_ready, t + 1)
                zt = zT[:, :, bass.ds(t * P, P)].rearrange("p c (b s) -> p c b s", b=BT)
                dve.tensor_reduce(zsum[:, :, bass.ds(t * BT, BT)], zt, AX.X, ALU.add).then_inc(zs_ready, 1)

            dve.wait_ge(x_done, 2 * T)
            norm_step(0)
            with dve.Fori(1, T) as t:
                norm_step(t)

            dve.wait_ge(gate_pe, 1)
            dve.tensor_scalar(logit[:, 0:E], bank[4][0:B, 0:E], 1.0 / S, None, ALU.mult).then_inc(gate_dve, 1)
            dve.wait_ge(gate_dve, 1)
            dve.max(top[:], logit[:]).then_inc(gate_dve, 1)
            dve.wait_ge(gate_dve, 2)
            dve.tensor_scalar(ntop[:], top[:, 0:1], -1.0, None, ALU.mult).then_inc(gate_dve, 1)
            dve.wait_ge(gate_act, 1)
            dve.reciprocal(exs[:, 1:2], exs[:, 0:1]).then_inc(gate_dve, 1)
            dve.wait_ge(gate_dve, 4)
            dve.tensor_scalar(prob[:, 0:E], ex[:], exs[:, 1:2], None, ALU.mult).then_inc(gate_dve, 1)
            dve.wait_ge(gate_dve, 5)
            dve.max(p8[:], prob[:]).then_inc(gate_dve, 1)
            dve.wait_ge(gate_dve, 6)
            dve.max_index(i8[:], p8[:], prob[:]).then_inc(gate_dve, 1)
            dve.tensor_tensor(cs[:, 0:1], p8[:, 0:1], p8[:, 1:2], ALU.add).then_inc(gate_dve, 1)
            dve.wait_ge(gate_dve, 8)
            dve.reciprocal(cs[:, 1:2], cs[:, 0:1]).then_inc(gate_dve, 1)
            dve.tensor_copy(i8f[:], i8[:, 0:TOPK]).then_inc(gate_dve, 1)
            dve.wait_ge(gate_dve, 10)
            dve.tensor_scalar(cw[:], p8[:, 0:TOPK], cs[:, 1:2], None, ALU.mult).then_inc(gate_dve, 1)
            for k in range(TOPK):
                ins = dve.tensor_scalar(pick[:, k, :], const[0:B, C_IOTA:C_IOTA + E], i8f[:, k:k + 1], None, ALU.is_equal)
            ins.then_inc(gate_dve, 1)
            dve.wait_ge(gate_dve, 12)
            dve.tensor_tensor(ctile[:], const[0:B, C_TILE:C_TILE + T].unsqueeze(2).to_broadcast([B, T, TOPK]),
                              cw[:].unsqueeze(1).to_broadcast([B, T, TOPK]), ALU.mult).then_inc(gate_dve, 1)
            dve.wait_ge(gate_pe, 2)
            dve.tensor_copy(pickT[:].rearrange("e k b -> e (k b)"), bank[5][0:E, 0:TOPK * B]).then_inc(gate_dve, 1)
            dve.wait_ge(gate_pe, 3)
            dve.tensor_copy(ctok[:].rearrange("p t k -> p (t k)"), bank[4][:, 0:T * TOPK]).then_inc(gate_dve, 1)
            dve.wait_ge(gate_pe, 4)
            dve.tensor_copy(b1s[:].rearrange("p b k a -> p a k b"),
                            bank[6][0:FH, 0:2 * TOPK * B].rearrange("p (a k b) -> p a k b", a=2, k=TOPK)).then_inc(gate_dve, 1)
            dve.wait_ge(gate_dve, 16)

            def expert_step(j, i, load, up, down):
                if up:
                    t = j - 1
                    dve.wait_ge(h_done, t + 1)
                    reached(dve, hT_ready, t)
                    bias = b1s[:, bass.ds(t * BT, BT), :, :].rearrange("p b k a -> p (b k a)")
                    dve.tensor_tensor(hb[:], bank[(i + 1) % 2][0:FH, :].rearrange("p (n t) -> p n t", t=S),
                                      bias.unsqueeze(2).to_broadcast([FH, BT * TOPK * 2, S]), ALU.add).then_inc(hb_ready, 1)
                if down:
                    t = j - 2
                    ct = tile_of(ctok, t)
                    dve.wait_ge(y_done, t + 1)
                    reached(dve, res_ready, t)
                    dve.scalar_tensor_tensor(out=part[:], in0=bank[2][:, 0:H], scalar=ct[:, 0:1], in1=tile_of(X, t),
                                             op0=ALU.mult, op1=ALU.add).then_inc(part_ready, 1)
                    dve.wait_ge(part_ready, t + 1)
                    if not isinstance(j, int) or j > 3:
                        dve.wait_ge(stored[i], 8 * (t - i))
                    dve.scalar_tensor_tensor(out=res[i][:], in0=bank[2][:, H:2 * H], scalar=ct[:, 1:2], in1=part[:],
                                             op0=ALU.mult, op1=ALU.add).then_inc(res_ready, 1)

            expert_steps(dve, expert_step)

        @block.tensor
        def _(pe):
            pe.wait_ge(w_in, 16 * (N_W + 2))
            pe.wait_ge(c_in, 16)
            pe.wait_ge(bias_b, 2)
            pe.matmul(bank[3][:, 0:H], ones[0:1, :], bout_row[:], start=True, stop=False)
            for h in range(2):
                ins = pe.matmul(bank[3][:, 0:H], bvb[:, h, :], wo_sb[SELF][:, h, :], start=False, stop=(h == 1))
            ins.then_inc(bias_mm, 1)
            pe.wait_ge(setup_pool, 10)

            def step(j, i, ln, la, lb, lc):
                if lc is not None:
                    t = j - 2
                    for c in range(KC):
                        pe.wait_ge(pr_ready[c], t + 1)
                        reached(pe, pT_ready[c], t)
                        for r in range(HQ):
                            ins = pe.transpose(bank[c][:, r * P:(r + 1) * P], pr[c][:, r, :, :].rearrange("p b k -> p (b k)"), ident)
                        ins.then_inc(t_done[c], 1)
                if la is not None:
                    pe.wait_ge(xn_ready, j + 1)
                    reached(pe, oT_ready, j - 2)
                    for c in range(KC):
                        ins = pe.transpose(bank[2][:, c * P:(c + 1) * P], xn[:, c * P:(c + 1) * P], ident)
                    ins.then_inc(x_done, 1)
                if lc is not None:
                    pe.wait_ge(v_ready, t + 1)
                    if isinstance(j, int) and j == 2:
                        pe.wait_ge(bias_ready, 1)
                    reached(pe, x_ready, t)
                    for c in range(KC):
                        pe.wait_ge(pT_ready[c], t + 1)
                        for r in range(HQ):
                            for h in range(2):
                                hp = c * HQ + r
                                ins = pe.matmul(bank[3][h * S:(h + 1) * S, hp * BT * VW:(hp + 1) * BT * VW],
                                                pT[c][:, r, h * S:(h + 1) * S],
                                                vd[i][:, 2 * hp + h, :, :].rearrange("p b d -> p (b d)"), start=True, stop=True)
                    ins.then_inc(pv_done, 1)
                if lb is not None:
                    t = j - 1
                    pe.wait_ge(q_ready, t + 1)
                    pe.wait_ge(kd_ready, 16 * HQ * (t + 1))
                    for c in range(KC):
                        reached(pe, masked[c], t)
                        for b in range(BT):
                            ins = pe.matmul(bank[4 + c][:, b * HQ * S:(b + 1) * HQ * S], qm[:, c, b, :, :].rearrange("p h q -> p (h q)"),
                                            kd[:, c, :, b * S:(b + 1) * S], start=True, stop=True)
                        ins.then_inc(s_done[c], 1)
                if lc is not None:
                    t = j - 2
                    pe.wait_ge(on_ready, t + 1)
                    if la is not None:
                        pe.wait_ge(xT_ready, j + 1)
                    for b in range(BT):
                        ins = pe.transpose(bank[2][:, b * P:(b + 1) * P], on[:, b, :, :].rearrange("p h d -> p (h d)"), ident)
                    ins.then_inc(o_done, 1)
                if la is not None:
                    if isinstance(j, int) and j == T:
                        pe.wait_ge(cross_in, 16 * 3)
                    wq, wk = (wqkv_sb[:, :, 0:H], wqkv_sb[:, :, H:2 * H]) if la == SELF else (wx["q"][:], wx["k"][:])
                    wv = wqkv_sb[:, :, 2 * H:3 * H] if la == SELF else wx["v"][:]
                    if la == SELF:
                        source = xnT[:]
                    else:
                        source = cT[i][:]
                    pe.wait_ge(xT_ready, j + 1)
                    reached(pe, q_ready, j)
                    if la == CROSS:
                        reached(pe, th_ready, j - T)
                    for o in range(KC):
                        for c in range(KC):
                            ins = pe.matmul(bank[6][:, o * P:(o + 1) * P], wq[:, c, o * P:(o + 1) * P], xnT[:, c, :],
                                            start=(c == 0), stop=(c == KC - 1))
                    ins.then_inc(q_done, 1)
                    if la == CROSS:
                        pe.wait_ge(ctx_in[i], 8 * (j - (T + i)) + 16)
                    reached(pe, v_ready, j)
                    for o in range(KC):
                        for c in range(KC):
                            ins = pe.matmul(bank[7][:, o * P:(o + 1) * P], wk[:, c, o * P:(o + 1) * P], source[:, c, :],
                                            start=(c == 0), stop=(c == KC - 1))
                    ins.then_inc(k_done, 1)
                    pe.wait_ge(k_ready, j + 1)
                    for c in range(KC):
                        ins = pe.matmul(bank[7][:, H:2 * H], source[:, c, :], wv[:, c, :], start=(c == 0), stop=(c == KC - 1))
                    ins.then_inc(v_done, 1)
                if lc is not None:
                    pe.wait_ge(oT_ready, t + 1)
                    for h in range(2):
                        ins = pe.matmul(bank[3][:, 0:H], oT[:, h, :, :].rearrange("p b q -> p (b q)"), wo_sb[lc][:, h, :], start=(h == 0), stop=(h == 1))
                    ins.then_inc(wo_done, 1)
                if la == CROSS:
                    pe.wait_ge(q_ready, j + 1)
                    for c in range(KC):
                        ins = pe.matmul(bank[6][:, H:2 * H], xnT[:, c, :], wx["g"][:, c, :], start=(c == 0), stop=(c == KC - 1))
                    ins.then_inc(g_done, 1)

            attention_steps(pe, step)

            def norm_step(t):
                pe.wait_ge(z_ready, t + 1)
                reached(pe, zT_ready, t)
                for c in range(KC):
                    ins = pe.transpose(bank[2][:, c * P:(c + 1) * P], xn[:, c * P:(c + 1) * P], ident)
                ins.then_inc(zt_done, 1)

            pe.wait_ge(oT_ready, 2 * T)
            norm_step(0)
            with pe.Fori(1, T) as t:
                norm_step(t)

            pe.wait_ge(zs_ready, T)
            pe.wait_ge(ffn_in, 16 * N_FFN)
            for c in range(KC):
                ins = pe.matmul(bank[4][0:B, 0:E], zsum[:, c, :], gw_sb[:, c, :], start=(c == 0), stop=(c == KC - 1))
            ins.then_inc(gate_pe, 1)
            pe.wait_ge(gate_dve, 13)
            for k in range(TOPK):
                ins = pe.transpose(bank[5][0:E, k * B:(k + 1) * B], pick[:, k, :], ident[0:B, 0:B])
            ins.then_inc(gate_pe, 1)
            pe.matmul(bank[4][:, 0:T * TOPK], const[0:B, C_SPREAD:C_SPREAD + P], ctile[:].rearrange("p t k -> p (t k)"),
                      start=True, stop=True).then_inc(gate_pe, 1)
            pe.wait_ge(gate_dve, 14)
            for a in range(2):
                ins = pe.matmul(bank[6][0:FH, a * TOPK * B:(a + 1) * TOPK * B], b1_sb[:, a * FH:(a + 1) * FH],
                                pickT[:].rearrange("e k b -> e (k b)"), start=True, stop=True)
            ins.then_inc(gate_pe, 1)

            def expert_step(j, i, load, up, down):
                if load:
                    pe.wait_ge(w_copied[i], 16 * BT * TOPK * 2 // 2 * (j - i) + 16 * BT * TOPK * 2)
                    reached(pe, hb_ready, j - 1)
                    for b in range(BT):
                        zb = zT[:, :, bass.ds(j * P + b * S, S)]
                        for k in range(TOPK):
                            for a in range(2):
                                n = (b * TOPK + k) * 2 + a
                                for c in range(KC):
                                    ins = pe.matmul(bank[i][0:FH, n * S:(n + 1) * S], w1c[i][:, b, k, c, a * FH:(a + 1) * FH],
                                                    zb[:, c, :], start=(c == 0), stop=(c == KC - 1))
                    ins.then_inc(h_done, 1)
                if up:
                    t = j - 1
                    pe.wait_ge(hT_ready, t + 1)
                    reached(pe, res_ready, t)
                    for k in range(TOPK):
                        for a in range(2):
                            for b in range(BT):
                                n = (b * TOPK + k) * 2 + a
                                K = FH + 1 if a == 0 else FH
                                ins = pe.matmul(bank[2][b * S:(b + 1) * S, k * H:(k + 1) * H], hT[0:K, n, :],
                                                w2c[1 - i][0:K, b, k, a, :], start=(a == 0), stop=(a == 1))
                    ins.then_inc(y_done, 1)

            expert_steps(pe, expert_step)


def kernel(x, ctx_2048, mask_BxS2_bk0, L0_attn_Wqkv, L0_attn_bqkv, L0_attn_Wout, L0_attn_bout, L0_xattn_norm_w,
           L0_xattn_wq, L0_xattn_wk, L0_xattn_wv, L0_xattn_wo, L0_xattn_wg, L0_ffn_gate_W, L0_ffn_W1, L0_ffn_b1,
           L0_ffn_W2, L0_ffn_b2):
    import concourse.bacc as _bacc
    from concourse.bass_utils import run_bass_kernel_spmd as _run

    def turned(w):
        return np.ascontiguousarray(np.asarray(w).T)

    def by_heads(w):
        return np.ascontiguousarray(np.asarray(w).T.reshape(HP, 2, HD, H).transpose(0, 2, 1, 3).reshape(P, 2, H))

    arrays = {
        "x": np.ascontiguousarray(np.asarray(x).reshape(B * S, H)),
        "ctxT": turned(np.asarray(ctx_2048).reshape(B * S, H)),
        "hidden": np.ascontiguousarray(np.asarray(mask_BxS2_bk0)).reshape(B * S),
        "consts": shape_constants(),
        "wqkvT": turned(L0_attn_Wqkv),
        "bqkv": np.ascontiguousarray(L0_attn_bqkv),
        "woutT": by_heads(L0_attn_Wout),
        "bout": np.ascontiguousarray(L0_attn_bout),
        "norm_w": np.ascontiguousarray(L0_xattn_norm_w),
        "wqT": turned(L0_xattn_wq),
        "wkT": turned(L0_xattn_wk),
        "wvT": turned(L0_xattn_wv),
        "woT": by_heads(L0_xattn_wo),
        "wgT": turned(L0_xattn_wg),
        "gateT": turned(L0_ffn_gate_W),
        "w1": np.ascontiguousarray(L0_ffn_W1),
        "b1": np.ascontiguousarray(L0_ffn_b1),
        "w2": np.ascontiguousarray(L0_ffn_W2),
        "b2": np.ascontiguousarray(L0_ffn_b2),
    }
    nc = _bacc.Bacc("TRN2", target_bir_lowering=False, num_devices=1)
    args = [nc.dram_tensor(n, a.shape, mybir.dt.from_np(a.dtype), kind="ExternalInput").ap() for n, a in arrays.items()]
    out = nc.dram_tensor("out", (B * S, H), F32, kind="ExternalOutput").ap()
    decoder_layer(nc, *args, out)
    r = _run(nc, [arrays], core_ids=[0])
    return np.asarray(r.results[0]["out"]).reshape(B, S, H)
```

```python
from contextlib import ExitStack

import numpy as np

import concourse.bass as bass
from concourse import mybir

ALU = mybir.AluOpType
ACT = mybir.ActivationFunctionType
AX = mybir.AxisListType
F32 = mybir.dt.float32
U32 = mybir.dt.uint32
U8 = mybir.dt.uint8

B, S, H = 32, 64, 256
NH, HD = 16, 16
E, F, TOPK = 6, 176, 2
P = 128
KC = H // P
BT = P // S
T = B // BT
HP = NH // 2
HQ = P // (2 * HD)
FH = F // 2
VW = HD + 1
SELF, CROSS = 0, 1
HIDDEN = -1e30
FLOOR = -1e29
LN_EPS, RMS_EPS = 1e-5, 1e-6

C_IDENT = 0
C_CAUSAL = C_IDENT + P
C_HEADS = C_CAUSAL + S
C_IOTA = C_HEADS + 2 * S
C_TILE = C_IOTA + E
C_SPREAD = C_TILE + T
C_END = C_SPREAD + P


def shape_constants():
    c = np.zeros((P, C_END), np.float32)
    p = np.arange(P)
    c[:, C_IDENT:C_IDENT + P] = np.eye(P)
    c[:, C_CAUSAL:C_CAUSAL + S] = np.where(np.arange(S)[None] > (p % S)[:, None], HIDDEN, 0.0)
    for odd in range(2):
        c[:, C_HEADS + odd * S:C_HEADS + (odd + 1) * S] = ((p // HD % 2 == odd) * HD ** -0.5)[:, None]
    c[:, C_IOTA:C_IOTA + E] = np.arange(E)
    c[:B, C_TILE:C_TILE + T] = (p[:B, None] // BT == np.arange(T)[None])
    c[:B, C_SPREAD:C_SPREAD + P] = (p[:B, None] % BT == (p // S)[None])
    return c


def decoder_layer(nc, x, ctxT, hidden, consts, wqkvT, bqk_cols, bv_cols, woutT, bout, nw_cols, wqT, wkT, wvT, woT, wgT,
                  gateT, w1, b1, w2, b2, out):
    ctx = ExitStack()
    with ctx:
        def sb(name, shape, dt=F32):
            return ctx.enter_context(nc.sbuf_tensor(name, shape, dt))

        def sem(name):
            return ctx.enter_context(nc.semaphore(name))

        bank = [ctx.enter_context(nc.psum_tensor(f"bank{i}", [P, 512], F32)) for i in range(8)]

        X = sb("X", [P, T, H])
        const = sb("const", [P, C_END])
        ident = const[:, C_IDENT:C_IDENT + P]
        causal = const[:, C_CAUSAL:C_CAUSAL + S]
        heads = const[:, C_HEADS:C_HEADS + 2 * S].rearrange("p (h q) -> p h q", h=2)
        ones = sb("ones", [P, P])
        minus_half = sb("minus_half", [P, 1])
        ln_eps = sb("ln_eps", [P, 1])
        rms_eps = sb("rms_eps", [P, 1])
        mf = [None] + [sb(f"mf{l}", [P, T, 2]) for l in (1, 2)]

        wqkv_sb = sb("wqkv_sb", [P, KC, 3 * H])
        bqk = sb("bqk", [P, 2 * KC])
        bv = sb("bv", [P, 2])
        bout_row = sb("bout_row", [1, H])
        wo_sb = [sb("wout_sb", [P, 2, H]), sb("wo_sb", [P, 2, H])]
        nw = sb("nw", [P, KC])
        wx = {n: sb(f"w{n}_sb", [P, KC, H]) for n in "qkvg"}
        bvb = sb("bvb", [P, 2, P])
        bias_rows = sb("bias_rows", [P, H])
        cT = [sb(f"cT{i}", [P, KC, P]) for i in range(2)]
        hid8 = sb("hid8", [P, B * S], U8)
        hide = sb("hide", [P, B * S])

        six0 = sb("six0", [P, 6])
        mv0 = sb("mv0", [P, 4])
        six1 = sb("six1", [P, 6])
        mv1 = sb("mv1", [P, 4])
        xn = sb("xn", [P, H])
        xnT = sb("xnT", [P, KC, P])
        zn = sb("zn", [P, H])
        qm = sb("qm", [P, KC, BT, 2, S])
        kd = sb("kd", [P, KC, HQ, P])
        vd = [sb(f"vd{i}", [P, NH, BT, VW]) for i in range(2)]
        th = [sb(f"th{i}", [P, H]) for i in range(2)]
        sm = [sb(f"sm{c}", [P, HQ, BT, S]) for c in range(KC)]
        mx = [sb(f"mx{c}", [P, BT * HQ]) for c in range(KC)]
        pr = [sb(f"pr{c}", [P, HQ, BT, S]) for c in range(KC)]
        pT = [sb(f"pT{c}", [P, HQ, P]) for c in range(KC)]
        rsum = sb("rsum", [P, HP, BT])
        rinv = sb("rinv", [P, HP, BT])
        on = sb("on", [P, BT, HP, HD])
        oT = sb("oT", [P, 2, BT, S])
        gated = sb("gated", [P, H])

        w1_sb = sb("w1_sb", [P, E, KC, F])
        w2_sb = sb("w2_sb", [FH + 1, E, 2, H])
        b1_sb = sb("b1_sb", [E, F])
        gw_sb = sb("gw_sb", [P, KC, E])
        zT = sb("zT", [P, KC, B * S])
        zsum = sb("zsum", [P, KC, B])
        zd = [sb(f"zd{i}", [P, KC, BT, P]) for i in range(2)]
        logit = sb("logit", [B, 8])
        top = sb("top", [B, 8])
        ntop = sb("ntop", [B, 1])
        ex = sb("ex", [B, E])
        exs = sb("exs", [B, 2])
        prob = sb("prob", [B, 8])
        p8 = sb("p8", [B, 8])
        i8 = sb("i8", [B, 8], U32)
        i8f = sb("i8f", [B, TOPK])
        cs = sb("cs", [B, 2])
        cw = sb("cw", [B, TOPK])
        pick = sb("pick", [B, TOPK, E])
        pickT = sb("pickT", [E, TOPK, B])
        ctile = sb("ctile", [B, T, TOPK])
        ctok = sb("ctok", [P, T, TOPK])
        irow = sb("irow", [1, B * TOPK], U32)
        b1s = sb("b1s", [FH, B, TOPK, 2])
        hs = sb("hs", [P, TOPK * 2, FH])
        hb = sb("hb", [FH, TOPK * 2, P])
        hd = sb("hd", [FH + 1, TOPK * 2, BT, P])
        part = sb("part", [P, H])
        res = [sb(f"res{i}", [P, H]) for i in range(2)]

        x_in0, x_in1, c_in, qkv_in, w_in, cross_in, ffn_in = (
            sem(n) for n in ("x_in0", "x_in1", "c_in", "qkv_in", "w_in", "cross_in", "ffn_in"))
        ctx_in = [sem(f"ctx_in{i}") for i in range(2)]
        setup_pool, setup_dve, bias_mm, bias_b, bias_ready = (
            sem(n) for n in ("setup_pool", "setup_dve", "bias_mm", "bias_b", "bias_ready"))
        six0_ready, mv0_ready, factor0 = sem("six0_ready"), sem("mv0_ready"), sem("factor0")
        six1_ready, mv1_ready = sem("six1_ready"), sem("mv1_ready")
        factor1 = [sem(f"factor1_{l}") for l in range(2)]
        mf_ready = [None] + [sem(f"mf_ready{l}") for l in (1, 2)]
        xn_ready, xb_ready = sem("xn_ready"), sem("xb_ready")
        x_done, xT_ready = sem("x_done"), sem("xT_ready")
        q_done, k_done, v_done, g_done = (sem(n) for n in ("q_done", "k_done", "v_done", "g_done"))
        q_ready, v_ready, th_ready = (
            sem(n) for n in ("q_ready", "v_ready", "th_ready"))
        kd_ready = [sem(f"kd_ready{c}") for c in range(KC)]
        s_done = [sem(f"s_done{c}") for c in range(KC)]
        masked = [sem(f"masked{c}") for c in range(KC)]
        mx_ready = [sem(f"mx_ready{c}") for c in range(KC)]
        mx_kept = [sem(f"mx_kept{c}") for c in range(KC)]
        less = [sem(f"less{c}") for c in range(KC)]
        pr_ready = [sem(f"pr_ready{c}") for c in range(KC)]
        t_done = [sem(f"t_done{c}") for c in range(KC)]
        pT_ready = [sem(f"pT_ready{c}") for c in range(KC)]
        pv_done, sum_kept, sum_inv, on_ready = (sem(n) for n in ("pv_done", "sum_kept", "sum_inv", "on_ready"))
        o_done, oT_ready, wo_done, gate_done, x_ready = (
            sem(n) for n in ("o_done", "oT_ready", "wo_done", "gate_done", "x_ready"))
        z_ready, zt_done, zT_ready, zs_ready = (sem(n) for n in ("z_ready", "zt_done", "zT_ready", "zs_ready"))
        gate_dve, gate_pe, gate_act, irow_in = (sem(n) for n in ("gate_dve", "gate_pe", "gate_act", "irow_in"))
        zt_kept, h_done, hs_ready, ht_done, hb_ready, hd_ready, y_done, part_ready, res_ready = (
            sem(n) for n in ("zt_kept", "h_done", "hs_ready", "ht_done", "hb_ready", "hd_ready", "y_done", "part_ready", "res_ready"))
        stored = [sem(f"stored{i}") for i in range(2)]

        N_C, N_W, N_CROSS, N_FFN = 2, 6, 4, 6

        def reached(eng, s, n):
            if not isinstance(n, int) or n > 0:
                eng.wait_ge(s, n)

        def alone(eng, s):
            eng.wait_ge(s, 1)

        def held(eng, n):
            return n if isinstance(n, int) else eng.snap(eng.to_reg(n))

        def tile_of(buf, t):
            return buf[:, bass.ds(t, 1), :].rearrange("p a h -> p (a h)")

        def attention_steps(eng, step):
            step(-1, 1, SELF, None, None, None)
            step(0, 0, SELF, SELF, None, None)
            step(1, 1, SELF, SELF, SELF, None)
            step(2, 0, SELF, SELF, SELF, SELF)
            with eng.Fori(3, T - 2, 2) as j:
                step(j, 1, SELF, SELF, SELF, SELF)
                step(j + 1, 0, SELF, SELF, SELF, SELF)
            step(T - 1, 1, CROSS, SELF, SELF, SELF)
            step(T, 0, CROSS, CROSS, SELF, SELF)
            step(T + 1, 1, CROSS, CROSS, CROSS, SELF)
            step(T + 2, 0, CROSS, CROSS, CROSS, CROSS)
            step(T + 3, 1, CROSS, CROSS, CROSS, CROSS)
            step(T + 4, 0, CROSS, CROSS, CROSS, CROSS)
            with eng.Fori(T + 5, 2 * T - 2, 2) as j:
                step(j, 1, CROSS, CROSS, CROSS, CROSS)
                step(j + 1, 0, CROSS, CROSS, CROSS, CROSS)
            step(2 * T - 1, 1, None, CROSS, CROSS, CROSS)
            step(2 * T, 0, None, None, CROSS, CROSS)
            step(2 * T + 1, 1, None, None, None, CROSS)
            step(2 * T + 2, 0, None, None, None, None)
            step(2 * T + 3, 1, None, None, None, None)

        def z_tile(j, lc, behind):
            if not isinstance(j, int):
                return j - behind - T if lc == CROSS else None
            return j - behind - T if 0 <= j - behind - T < T else None

        def expert_steps(eng, step):
            step(0, 0, True, False, False)
            step(1, 1, True, True, False)
            step(2, 0, True, True, True)
            step(3, 1, True, True, True)
            with eng.Fori(4, T - 1, 2) as j:
                step(j, 0, True, True, True)
                step(j + 1, 1, True, True, True)
            step(T, 0, False, True, True)
            step(T + 1, 1, False, False, True)

        block = ctx.enter_context(nc.Block())

        @block.sync
        def _(sp):
            xt = x.rearrange("(t p) h -> p t h", p=P)
            sp.dma_start(X[:, 0:2, :], xt[:, 0:2, :]).then_inc(x_in0, 16)
            sp.dma_start(wqkv_sb[:], wqkvT.rearrange("(c p) o -> p c o", p=P)).then_inc(qkv_in, 16)
            sp.dma_start(X[:, 2:T, :], xt[:, 2:T, :]).then_inc(x_in1, 16)
            sp.dma_start(wo_sb[SELF][:], woutT).then_inc(w_in, 16)
            sp.dma_start(wx["q"][:], wqT.rearrange("(c p) o -> p c o", p=P)).then_inc(w_in, 16)
            sp.dma_start(wx["g"][:], wgT.rearrange("(c p) o -> p c o", p=P)).then_inc(w_in, 16)

            def step(j, i, ln, la, lb, lc):
                if la == CROSS:
                    if not isinstance(j, int) or j > T + 1:
                        sp.wait_ge(v_done, j - 1)
                    sp.dma_start(cT[i][:], ctxT.rearrange("(c p) n -> p c n", p=P)[:, :, bass.ds((j - T) * P, P)]
                                 ).then_inc(ctx_in[i], 16)
                if isinstance(j, int) and j == T:
                    sp.dma_start(w1_sb[:], w1.rearrange("e (c p) f -> p e c f", p=P)).then_inc(ffn_in, 16)
                    sp.dma_start(w2_sb[0:FH, :, :, :], w2.rearrange("e (a p) h -> p e a h", p=FH)).then_inc(ffn_in, 16)
                    for a in range(2):
                        sp.dma_start(w2_sb[FH:FH + 1, :, a, :], b2.rearrange("(q e) h -> q e h", q=1)).then_inc(ffn_in, 16)
                    sp.dma_start(b1_sb[:], b1).then_inc(ffn_in, 16)
                    sp.dma_start(gw_sb[:], gateT.rearrange("(c p) e -> p c e", p=P)).then_inc(ffn_in, 16)

            attention_steps(sp, step)

            sp.wait_ge(gate_dve, 7)
            sp.dma_start(irow[:], i8[:, 0:TOPK]).then_inc(irow_in, 16)

            def expert_step(j, i, load, up, down):
                if down:
                    sp.wait_ge(res_ready, j - 1)
                    sp.dma_start(out[bass.ds((j - 2) * P, P), :], res[i][:]).then_inc(stored[i], 16)

            expert_steps(sp, expert_step)
            for i in range(2):
                sp.wait_ge(stored[i], 16 * (T // 2))

        @block.gpsimd
        def _(pool):
            pool.memset(minus_half[:], -0.5).then_inc(setup_pool, 1)
            pool.memset(ln_eps[:], LN_EPS).then_inc(setup_pool, 1)
            pool.memset(rms_eps[:], RMS_EPS).then_inc(setup_pool, 1)
            pool.memset(kd[:], 0.0).then_inc(setup_pool, 1)
            for i in range(2):
                pool.memset(vd[i][:], 0.0).then_inc(setup_pool, 1)
            pool.wait_ge(setup_pool, 6)
            for i in range(2):
                for b in range(BT):
                    pool.memset(vd[i][b * S:(b + 1) * S, :, b, HD:VW], 1.0).then_inc(setup_pool, 1)
            pool.wait_ge(setup_pool, 10)

            def step(j, i, ln, la, lb, lc):
                def entering_factor():
                    n = j + 1
                    pool.wait_ge(mv0_ready, n + 1)
                    pool.tensor_tensor(mv0[:, 3:4], mv0[:, 1:2], ln_eps[:], ALU.add).then_inc(factor0, 1)
                    pool.wait_ge(factor0, 2 * n + 1)
                    pool.tensor_tensor(mv0[:, 2:3], mv0[:, 3:4], minus_half[:], ALU.pow).then_inc(factor0, 1)

                def less_max(c):
                    t = j - 1
                    maxima = held(pool, t + 1)
                    if lb == CROSS:
                        alone(pool, setup_pool)
                    pool.wait_ge(mx_ready[c], maxima)
                    if lb == CROSS:
                        pool.tensor_scalar(mx[c][:], mx[c][:], FLOOR, None, ALU.max).then_inc(mx_kept[c], 1)
                        pool.wait_ge(mx_kept[c], t - T + 1)
                    s3 = sm[c][:].rearrange("p h b k -> p (h b) k")
                    pool.tensor_tensor(s3, s3, mx[c][:].unsqueeze(2).to_broadcast([P, BT * HQ, S]), ALU.subtract
                                       ).then_inc(less[c], 1)

                if lb is not None:
                    for c in range(KC):
                        less_max(c)
                if ln == SELF:
                    entering_factor()
                if lb == SELF:
                    t = j - 1
                    alone(pool, setup_pool)
                    if isinstance(j, int) and j == 1:
                        pool.wait_ge(bias_ready, 1)
                    pool.wait_ge(xn_ready, t + 1)
                    pool.tensor_tensor(tile_of(X, t), tile_of(X, t), bias_rows[:], ALU.add).then_inc(xb_ready, 1)
                if lc is not None:
                    t = j - 2
                    u = t - lc * T
                    chain, a, r, f = factor1[lc], mv1[:, 3:4], mv1[:, 1:2], mv1[:, 2:3]
                    per = 7 if lc == SELF else 2
                    pool.wait_ge(mv1_ready, t + 1)
                    pool.tensor_tensor(a, r, ln_eps[:], ALU.add).then_inc(chain, 1)
                    pool.wait_ge(chain, per * u + 1)
                    pool.tensor_tensor(f, a, minus_half[:], ALU.pow).then_inc(chain, 1)
                    if lc == SELF:
                        pool.wait_ge(chain, per * u + 2)
                        pool.tensor_tensor(a, r, f, ALU.mult).then_inc(chain, 1)
                        pool.wait_ge(chain, per * u + 3)
                        pool.tensor_tensor(a, a, f, ALU.mult).then_inc(chain, 1)
                        pool.wait_ge(chain, per * u + 4)
                        pool.tensor_tensor(a, a, rms_eps[:], ALU.add).then_inc(chain, 1)
                        pool.wait_ge(chain, per * u + 5)
                        pool.tensor_tensor(a, a, minus_half[:], ALU.pow).then_inc(chain, 1)
                        pool.wait_ge(chain, per * u + 6)
                        pool.tensor_tensor(f, f, a, ALU.mult).then_inc(chain, 1)
                    alone(pool, setup_pool)
                    pool.wait_ge(chain, per * u + per)
                    pool.tensor_copy(tile_of(mf[lc + 1], u), mv1[:, 0:3:2]).then_inc(mf_ready[lc + 1], 1)

            attention_steps(pool, step)
            for i in range(2):
                pool.memset(zd[i][:], 0.0).then_inc(setup_pool, 1)
            pool.wait_ge(setup_pool, 12)

            def expert_step(j, i, load, up, down):
                if load:
                    alone(pool, setup_pool)
                    reached(pool, h_done, j - 1)
                    if isinstance(j, int) and j == 0:
                        pool.wait_ge(zT_ready, T)
                    own = zd[i][:].rearrange("p c b t -> p c (b t)")
                    for b in range(BT):
                        ins = pool.tensor_copy(own[:, :, b * (P + S):b * (P + S) + S], zT[:, :, bass.ds(j * P + b * S, S)])
                    ins.then_inc(zt_kept, 1)

            expert_steps(pool, expert_step)

        @block.scalar
        def _(act):
            act.dma_start(const[:], consts).then_inc(c_in, 16)
            act.dma_start(bqk[:], bqk_cols).then_inc(c_in, 16)
            act.dma_start(bv[:], bv_cols).then_inc(w_in, 16)
            act.dma_start(nw[:], nw_cols).then_inc(w_in, 16)
            act.dma_start(bout_row[:], bout.rearrange("(a h) -> a h", a=1)).then_inc(w_in, 16)
            act.dma_start(hid8[:], hidden.rearrange("(a n) -> a n", a=1).to_broadcast([P, B * S])).then_inc(cross_in, 16)
            act.dma_start(wx["k"][:], wkT.rearrange("(c p) o -> p c o", p=P)).then_inc(cross_in, 16)
            act.dma_start(wx["v"][:], wvT.rearrange("(c p) o -> p c o", p=P)).then_inc(cross_in, 16)
            act.dma_start(wo_sb[CROSS][:], woT).then_inc(cross_in, 16)

            def step(j, i, ln, la, lb, lc):
                if isinstance(j, int) and j == 0:
                    act.wait_ge(c_in, 16 * N_C)
                    act.wait_ge(setup_pool, 10)
                if isinstance(j, int) and j == 1:
                    act.wait_ge(bias_mm, 1)
                    act.copy(bias_rows[:], bank[3][:, 0:H]).then_inc(bias_ready, 1)
                if lc is not None:
                    t = j - 2
                    for c in range(KC):
                        act.wait_ge(t_done[c], t + 1)
                        reached(act, pv_done, t)
                        act.copy(pT[c][:].rearrange("p h q -> p (h q)"), bank[c][:]).then_inc(pT_ready[c], 1)
                def keys(layer, t, c):
                    if c == 0:
                        act.wait_ge(k_done, t + 1)
                        act.wait_ge(v_done, t + 1)
                    reached(act, s_done[c], t)
                    for r in range(HQ):
                        rows = slice(r * 2 * HD, (r + 1) * 2 * HD)
                        k = bank[7][rows, c * P:(c + 1) * P]
                        if layer == SELF:
                            ins = act.activation(kd[rows, c, r, :], k, ACT.Identity, bias=bqk[rows, KC + c:KC + c + 1])
                        else:
                            ins = act.copy(kd[rows, c, r, :], k)
                    ins.then_inc(kd_ready[c], 1)

                if lb is not None:
                    keys(lb, j - 1, 1)
                if la is not None:
                    act.wait_ge(x_done, j + 1)
                    reached(act, v_done, j)
                    if la == CROSS:
                        reached(act, g_done, j - T)
                    if z_tile(j, lc, 4) is not None:
                        act.wait_ge(zt_done, z_tile(j, lc, 4) + 1)
                    act.copy(xnT[:].rearrange("p c t -> p (c t)"), bank[2][:, 0:H]).then_inc(xT_ready, 1)
                tz = z_tile(j, lc, 4)
                if tz is not None:
                    alone(act, setup_dve)
                    act.wait_ge(zt_done, tz + 1)
                    act.copy(zT[:, :, bass.ds(tz * P, P)], bank[2][:, H:2 * H].rearrange("p (c t) -> p c t", c=KC)
                             ).then_inc(zT_ready, 1)

                def softmax(c):
                    t = j - 1
                    act.wait_ge(less[c], t + 1)
                    reached(act, t_done[c], t)
                    act.activation(pr[c][:].rearrange("p h b k -> p (h b k)"), sm[c][:].rearrange("p h b k -> p (h b k)"),
                                   ACT.Exp).then_inc(pr_ready[c], 1)

                if lb is not None:
                    softmax(0)
                if lc is not None:
                    t = j - 2
                    act.wait_ge(o_done, t + 1)
                    reached(act, wo_done, t)
                    act.copy(oT[:].rearrange("p h b q -> p b h q"), bank[2][:, 0:H].rearrange("p (b h q) -> p b h q", b=BT, h=2)
                             ).then_inc(oT_ready, 1)
                if la is not None:
                    keys(la, j, 0)
                if lb is not None:
                    softmax(1)
                if la is not None:
                    reached(act, pv_done, j - 1)
                    for b in range(BT):
                        rows = slice(b * S, (b + 1) * S)
                        ins = act.copy(vd[i][rows, :, b, 0:HD], bank[7][rows, H:2 * H].rearrange("p (h d) -> p h d", d=HD))
                    ins.then_inc(v_ready, 1)
                if la == CROSS:
                    act.wait_ge(g_done, j - T + 1)
                    reached(act, gate_done, j - T - 1)
                    act.activation(th[i][:], bank[6][:, H:2 * H], ACT.Tanh, scale=0.5).then_inc(th_ready, 1)

            attention_steps(act, step)

            act.wait_ge(gate_dve, 3)
            act.activation(ex[:], logit[:, 0:E], ACT.Exp, bias=ntop[:, 0:1], accum_out=exs[:, 0:1]).then_inc(gate_act, 1)

            def expert_step(j, i, load, up, down):
                if up:
                    t = j - 1
                    act.wait_ge(hb_ready, t + 1)
                    reached(act, y_done, t)
                    own = hd[0:FH, :, :, :].rearrange("p n b t -> p n (b t)")
                    for b in range(BT):
                        ins = act.activation(own[:, :, b * (P + S):b * (P + S) + S], hb[:, :, b * S:(b + 1) * S], ACT.Gelu)
                    ins.then_inc(hd_ready, 1)
                if load:
                    act.wait_ge(h_done, j + 1)
                    reached(act, ht_done, j)
                    act.copy(hs[:].rearrange("p n f -> p (n f)"), bank[i][:, 0:TOPK * F]).then_inc(hs_ready, 1)

            expert_steps(act, expert_step)

        @block.vector
        def _(dve):
            dve.memset(ones[:], 1.0).then_inc(setup_dve, 1)
            dve.memset(hd[:], 0.0).then_inc(setup_dve, 1)
            dve.memset(logit[:], HIDDEN).then_inc(setup_dve, 1)
            dve.memset(prob[:], -1.0).then_inc(setup_dve, 1)
            dve.wait_ge(setup_dve, 4)
            for b in range(BT):
                dve.memset(hd[P // 2:FH + 1, :, b, b * S:(b + 1) * S], 1.0).then_inc(setup_dve, 1)
            dve.wait_ge(setup_dve, 4 + BT)

            def fold():
                dve.wait_ge(w_in, 16 * N_W)
                for h in range(2):
                    ins = dve.tensor_scalar(bvb[:, h, :], ones[:], bv[:, h:h + 1], None, ALU.mult)
                ins.then_inc(bias_b, 1)
                for n in "qg":
                    for c in range(KC):
                        ins = dve.tensor_scalar(wx[n][:, c, :], wx[n][:, c, :], nw[:, c:c + 1], None, ALU.mult)
                ins.then_inc(bias_b, 1)

            def step(j, i, ln, la, lb, lc):
                if isinstance(j, int) and j == 1:
                    fold()
                def entering_stats():
                    n = j + 1
                    alone(dve, setup_dve)
                    if isinstance(j, int) and j < 2:
                        dve.wait_ge(*((x_in1, 16) if n > 1 else (x_in0, 16)))
                    reached(dve, mv0_ready, n)
                    dve.bn_stats(six0[:], tile_of(X, n)).then_inc(six0_ready, 1)

                def entering_mean():
                    n = j + 1
                    n1 = held(dve, n + 1)
                    alone(dve, setup_dve)
                    dve.wait_ge(six0_ready, n1)
                    reached(dve, xn_ready, n)
                    dve.bn_aggr(mv0[:, 0:2], six0[:]).then_inc(mv0_ready, 1)

                if isinstance(j, int) and j == T:
                    dve.wait_ge(cross_in, 16 * N_CROSS)
                    dve.tensor_scalar(hide[:], hid8[:], -1.0, -HIDDEN, ALU.add, ALU.mult).then_inc(setup_dve, 1)
                    dve.wait_ge(setup_dve, 7)
                def mask_and_max(c):
                    t = j - 1
                    scores = bank[4 + c][:].rearrange("p (b h k) -> p b h k", b=BT, h=HQ)
                    dve.wait_ge(s_done[c], t + 1)
                    reached(dve, pr_ready[c], t)
                    if lb == SELF:
                        m = causal.unsqueeze(1).to_broadcast([P, BT, S])
                    else:
                        m = hide[:, bass.ds((t - T) * P, P)].rearrange("p (b k) -> p b k", b=BT)
                    dve.tensor_tensor(sm[c][:].rearrange("p h b k -> p b h k"), scores,
                                      m.unsqueeze(2).to_broadcast([P, BT, HQ, S]), ALU.add).then_inc(masked[c], 1)
                    dve.wait_ge(masked[c], t + 1)
                    dve.tensor_reduce(mx[c][:], sm[c][:].rearrange("p h b k -> p (h b) k"), AX.X, ALU.max
                                      ).then_inc(mx_ready[c], 1)
                if lb is not None:
                    mask_and_max(0)
                if lc is not None:
                    t = j - 2
                    O = bank[3][:, 0:HP * BT * VW].rearrange("p (h b d) -> p h b d", h=HP, b=BT)
                    dve.wait_ge(pv_done, t + 1)
                    reached(dve, on_ready, t)
                    if lc == SELF:
                        dve.tensor_scalar(rsum[:], O[:, :, :, HD], 1.0, None, ALU.mult).then_inc(sum_kept, 1)
                    else:
                        dve.tensor_scalar(rsum[:], O[:, :, :, HD], 1e-30, 2.0, ALU.max, ALU.mult).then_inc(sum_kept, 1)
                    dve.wait_ge(sum_kept, t + 1)
                    dve.reciprocal(rinv[:], rsum[:]).then_inc(sum_inv, 1)
                    dve.wait_ge(sum_inv, t + 1)
                    reached(dve, o_done, t)
                    dve.tensor_tensor(on[:].rearrange("p b h d -> p h b d"), O[:, :, :, 0:HD],
                                      rinv[:].unsqueeze(3).to_broadcast([P, HP, BT, HD]), ALU.mult).then_inc(on_ready, 1)
                def queries():
                    if isinstance(j, int) and j == 0:
                        dve.wait_ge(c_in, 16 * N_C)
                    dve.wait_ge(q_done, j + 1)
                    reached(dve, s_done[1], j)
                    if la == SELF:
                        for c in range(KC):
                            for b in range(BT):
                                qc = bank[6][:, c * P + b * S:c * P + (b + 1) * S].unsqueeze(1).to_broadcast([P, 2, S])
                                ins = dve.scalar_tensor_tensor(out=qm[:, c, b, :, :], in0=qc, scalar=bqk[:, c:c + 1],
                                                               in1=heads, op0=ALU.add, op1=ALU.mult)
                    else:
                        qc = bank[6][:, 0:H].rearrange("p (n q) -> p n q", q=S)
                        ins = dve.tensor_tensor(qm[:].rearrange("p c b h q -> p (c b) h q"),
                                                qc.unsqueeze(2).to_broadcast([P, KC * BT, 2, S]),
                                                heads.unsqueeze(1).to_broadcast([P, KC * BT, 2, S]), ALU.mult)
                    ins.then_inc(q_ready, 1)

                if ln == SELF:
                    entering_stats()
                if lb is not None:
                    mask_and_max(1)
                if ln == SELF:
                    entering_mean()
                if la is not None:
                    queries()
                if ln is not None:
                    n = j + 1
                    reached(dve, x_done, n)
                    if ln == SELF:
                        dve.wait_ge(factor0, 2 * n + 2)
                        mean, factor = mv0[:, 0:1], mv0[:, 2:3]
                    else:
                        dve.wait_ge(mf_ready[1], n - T + 1)
                        mean, factor = tile_of(mf[1], n - T)[:, 0:1], tile_of(mf[1], n - T)[:, 1:2]
                    dve.tensor_scalar(xn[:], tile_of(X, n - ln * T), mean, factor, ALU.subtract, ALU.mult).then_inc(xn_ready, 1)
                tz = z_tile(j, lc, 3)
                if tz is not None:
                    m = tile_of(mf[2], tz)
                    dve.wait_ge(mf_ready[2], tz + 1)
                    reached(dve, zt_done, tz)
                    dve.tensor_scalar(zn[:], tile_of(X, tz), m[:, 0:1], m[:, 1:2], ALU.subtract, ALU.mult).then_inc(z_ready, 1)
                tz = z_tile(j, lc, 4)
                if tz is not None:
                    alone(dve, setup_dve)
                    dve.wait_ge(zT_ready, tz + 1)
                    zt = zT[:, :, bass.ds(tz * P, P)].rearrange("p c (b s) -> p c b s", b=BT)
                    dve.tensor_reduce(zsum[:, :, bass.ds(tz * BT, BT)], zt, AX.X, ALU.add).then_inc(zs_ready, 1)
                if lc is not None:
                    t = j - 2
                    xt = tile_of(X, t - lc * T)
                    wo = bank[3][:, 0:H]
                    dve.wait_ge(wo_done, t + 1)
                    if lc == SELF:
                        dve.wait_ge(xb_ready, t + 1)
                        dve.tensor_tensor(xt, wo, xt, ALU.add).then_inc(x_ready, 1)
                    else:
                        dve.wait_ge(th_ready, t - T + 1)
                        dve.scalar_tensor_tensor(out=gated[:], in0=th[i][:], scalar=1.0, in1=wo, op0=ALU.add, op1=ALU.mult
                                                 ).then_inc(gate_done, 1)
                        dve.wait_ge(gate_done, t - T + 1)
                        dve.tensor_tensor(xt, gated[:], xt, ALU.add).then_inc(x_ready, 1)
                    alone(dve, setup_dve)
                    dve.wait_ge(x_ready, t + 1)
                    dve.bn_stats(six1[:], xt).then_inc(six1_ready, 1)
                    if lc == SELF:
                        alone(dve, setup_dve)
                        reached(dve, mf_ready[1], t)
                    else:
                        dve.wait_ge(mf_ready[1], T)
                        reached(dve, mf_ready[2], t - T)
                    dve.wait_ge(six1_ready, t + 1)
                    dve.bn_aggr(mv1[:, 0:2], six1[:]).then_inc(mv1_ready, 1)

            attention_steps(dve, step)

            dve.wait_ge(gate_pe, 1)
            dve.tensor_scalar(logit[:, 0:E], bank[4][0:B, 0:E], 1.0 / S, None, ALU.mult).then_inc(gate_dve, 1)
            dve.wait_ge(gate_dve, 1)
            dve.max(top[:], logit[:]).then_inc(gate_dve, 1)
            dve.wait_ge(gate_dve, 2)
            dve.tensor_scalar(ntop[:], top[:, 0:1], -1.0, None, ALU.mult).then_inc(gate_dve, 1)
            dve.wait_ge(gate_act, 1)
            dve.reciprocal(exs[:, 1:2], exs[:, 0:1]).then_inc(gate_dve, 1)
            dve.wait_ge(gate_dve, 4)
            dve.tensor_scalar(prob[:, 0:E], ex[:], exs[:, 1:2], None, ALU.mult).then_inc(gate_dve, 1)
            dve.wait_ge(gate_dve, 5)
            dve.max(p8[:], prob[:]).then_inc(gate_dve, 1)
            dve.wait_ge(gate_dve, 6)
            dve.max_index(i8[:], p8[:], prob[:]).then_inc(gate_dve, 1)
            dve.tensor_tensor(cs[:, 0:1], p8[:, 0:1], p8[:, 1:2], ALU.add).then_inc(gate_dve, 1)
            dve.wait_ge(gate_dve, 8)
            dve.reciprocal(cs[:, 1:2], cs[:, 0:1]).then_inc(gate_dve, 1)
            dve.tensor_copy(i8f[:], i8[:, 0:TOPK]).then_inc(gate_dve, 1)
            dve.wait_ge(gate_dve, 10)
            dve.tensor_scalar(cw[:], p8[:, 0:TOPK], cs[:, 1:2], None, ALU.mult).then_inc(gate_dve, 1)
            for k in range(TOPK):
                ins = dve.tensor_scalar(pick[:, k, :], const[0:B, C_IOTA:C_IOTA + E], i8f[:, k:k + 1], None, ALU.is_equal)
            ins.then_inc(gate_dve, 1)
            dve.wait_ge(gate_dve, 12)
            dve.tensor_tensor(ctile[:], const[0:B, C_TILE:C_TILE + T].unsqueeze(2).to_broadcast([B, T, TOPK]),
                              cw[:].unsqueeze(1).to_broadcast([B, T, TOPK]), ALU.mult).then_inc(gate_dve, 1)
            dve.wait_ge(gate_pe, 2)
            dve.tensor_copy(pickT[:].rearrange("e k b -> e (k b)"), bank[5][0:E, 0:TOPK * B]).then_inc(gate_dve, 1)
            dve.wait_ge(gate_pe, 3)
            dve.tensor_copy(ctok[:].rearrange("p t k -> p (t k)"), bank[4][:, 0:T * TOPK]).then_inc(gate_dve, 1)
            dve.wait_ge(gate_pe, 4)
            dve.tensor_copy(b1s[:].rearrange("p b k a -> p a k b"),
                            bank[6][0:FH, 0:2 * TOPK * B].rearrange("p (a k b) -> p a k b", a=2, k=TOPK)).then_inc(gate_dve, 1)
            dve.wait_ge(gate_dve, 16)

            def expert_step(j, i, load, up, down):
                if up:
                    t = j - 1
                    dve.wait_ge(ht_done, t + 1)
                    reached(dve, hd_ready, t)
                    for b in range(BT):
                        bias = b1s[:, bass.ds(t * BT + b, 1), :, :].rearrange("p b k a -> p (b k a)")
                        ins = dve.tensor_tensor(hb[:, :, b * S:(b + 1) * S],
                                                bank[2][0:FH, :].rearrange("p (n t) -> p n t", t=P)[:, :, b * S:(b + 1) * S],
                                                bias.unsqueeze(2).to_broadcast([FH, TOPK * 2, S]), ALU.add)
                    ins.then_inc(hb_ready, 1)
                if down:
                    t = j - 2
                    ct = tile_of(ctok, t)
                    dve.wait_ge(y_done, t + 1)
                    reached(dve, res_ready, t)
                    y = bank[4 + i]
                    dve.scalar_tensor_tensor(out=part[:], in0=y[:, 0:H], scalar=ct[:, 0:1], in1=tile_of(X, t),
                                             op0=ALU.mult, op1=ALU.add).then_inc(part_ready, 1)
                    dve.wait_ge(part_ready, t + 1)
                    if not isinstance(j, int) or j > 3:
                        dve.wait_ge(stored[i], 8 * (t - i))
                    dve.scalar_tensor_tensor(out=res[i][:], in0=y[:, H:2 * H], scalar=ct[:, 1:2], in1=part[:],
                                             op0=ALU.mult, op1=ALU.add).then_inc(res_ready, 1)

            expert_steps(dve, expert_step)

        @block.tensor
        def _(pe):
            def constant_output():
                pe.wait_ge(w_in, 16 * N_W)
                pe.wait_ge(bias_b, 2)
                pe.matmul(bank[3][:, 0:H], ones[0:1, :], bout_row[:], start=True, stop=False)
                for h in range(2):
                    ins = pe.matmul(bank[3][:, 0:H], bvb[:, h, :], wo_sb[SELF][:, h, :], start=False, stop=(h == 1))
                ins.then_inc(bias_mm, 1)

            pe.wait_ge(c_in, 16 * N_C)

            def step(j, i, ln, la, lb, lc):
                if lc is not None:
                    t = j - 2
                    for c in range(KC):
                        pe.wait_ge(pr_ready[c], t + 1)
                        reached(pe, pT_ready[c], t)
                        for r in range(HQ):
                            ins = pe.transpose(bank[c][:, r * P:(r + 1) * P], pr[c][:, r, :, :].rearrange("p b k -> p (b k)"), ident)
                        ins.then_inc(t_done[c], 1)
                if la is not None:
                    pe.wait_ge(xn_ready, j + 1)
                    reached(pe, oT_ready, j - 2)
                    for c in range(KC):
                        ins = pe.transpose(bank[2][:, c * P:(c + 1) * P], xn[:, c * P:(c + 1) * P], ident)
                    ins.then_inc(x_done, 1)
                tz = z_tile(j, lc, 4)
                if tz is not None:
                    pe.wait_ge(z_ready, tz + 1)
                    reached(pe, zT_ready, tz)
                    for c in range(KC):
                        ins = pe.transpose(bank[2][:, H + c * P:H + (c + 1) * P], zn[:, c * P:(c + 1) * P], ident)
                    ins.then_inc(zt_done, 1)

                def scores(c):
                    t = j - 1
                    if c == 0:
                        pe.wait_ge(q_ready, t + 1)
                    pe.wait_ge(kd_ready[c], t + 1)
                    reached(pe, masked[c], t)
                    for b in range(BT):
                        ins = pe.matmul(bank[4 + c][:, b * HQ * S:(b + 1) * HQ * S], qm[:, c, b, :, :].rearrange("p h q -> p (h q)"),
                                        kd[:, c, :, b * S:(b + 1) * S], start=True, stop=True)
                    ins.then_inc(s_done[c], 1)

                if lb is not None:
                    scores(0)
                if lc is not None:
                    t = j - 2
                    pe.wait_ge(v_ready, t + 1)
                    if isinstance(j, int) and j == 2:
                        pe.wait_ge(bias_ready, 1)
                    reached(pe, x_ready, t)
                    for c in range(KC):
                        pe.wait_ge(pT_ready[c], t + 1)
                        for r in range(HQ):
                            for h in range(2):
                                hp = c * HQ + r
                                ins = pe.matmul(bank[3][h * S:(h + 1) * S, hp * BT * VW:(hp + 1) * BT * VW],
                                                pT[c][:, r, h * S:(h + 1) * S],
                                                vd[i][:, 2 * hp + h, :, :].rearrange("p b d -> p (b d)"), start=True, stop=True)
                    ins.then_inc(pv_done, 1)
                if lb is not None:
                    scores(1)
                if la is not None:
                    if isinstance(j, int) and j == 0:
                        pe.wait_ge(qkv_in, 16)
                    if isinstance(j, int) and j == T:
                        pe.wait_ge(cross_in, 16 * N_CROSS)
                    wq, wk = (wqkv_sb[:, :, 0:H], wqkv_sb[:, :, H:2 * H]) if la == SELF else (wx["q"][:], wx["k"][:])
                    wv = wqkv_sb[:, :, 2 * H:3 * H] if la == SELF else wx["v"][:]
                    source = xnT[:] if la == SELF else cT[i][:]
                    pe.wait_ge(xT_ready, j + 1)
                    if la == CROSS:
                        pe.wait_ge(ctx_in[i], 8 * (j - (T + i)) + 16)
                    reached(pe, kd_ready[1], j)
                    reached(pe, v_ready, j)
                    for o in range(KC):
                        for c in range(KC):
                            ins = pe.matmul(bank[7][:, o * P:(o + 1) * P], wk[:, c, o * P:(o + 1) * P], source[:, c, :],
                                            start=(c == 0), stop=(c == KC - 1))
                    ins.then_inc(k_done, 1)
                    for c in range(KC):
                        ins = pe.matmul(bank[7][:, H:2 * H], source[:, c, :], wv[:, c, :], start=(c == 0), stop=(c == KC - 1))
                    ins.then_inc(v_done, 1)
                if lc is not None:
                    t = j - 2
                    pe.wait_ge(on_ready, t + 1)
                    if la is not None:
                        pe.wait_ge(xT_ready, j + 1)
                    if tz is not None:
                        pe.wait_ge(zT_ready, tz + 1)
                    for b in range(BT):
                        ins = pe.transpose(bank[2][:, b * P:(b + 1) * P], on[:, b, :, :].rearrange("p h d -> p (h d)"), ident)
                    ins.then_inc(o_done, 1)
                if la is not None:
                    reached(pe, q_ready, j)
                    if la == CROSS:
                        reached(pe, th_ready, j - T)
                    for o in range(KC):
                        for c in range(KC):
                            ins = pe.matmul(bank[6][:, o * P:(o + 1) * P], wq[:, c, o * P:(o + 1) * P], xnT[:, c, :],
                                            start=(c == 0), stop=(c == KC - 1))
                    ins.then_inc(q_done, 1)
                if lc is not None:
                    pe.wait_ge(oT_ready, t + 1)
                    for h in range(2):
                        ins = pe.matmul(bank[3][:, 0:H], oT[:, h, :, :].rearrange("p b q -> p (b q)"), wo_sb[lc][:, h, :],
                                        start=(h == 0), stop=(h == 1))
                    ins.then_inc(wo_done, 1)
                if la == CROSS:
                    pe.wait_ge(q_ready, j + 1)
                    for c in range(KC):
                        ins = pe.matmul(bank[6][:, H:2 * H], xnT[:, c, :], wx["g"][:, c, :], start=(c == 0), stop=(c == KC - 1))
                    ins.then_inc(g_done, 1)
                if isinstance(j, int) and j == 0:
                    constant_output()

            attention_steps(pe, step)

            pe.wait_ge(zs_ready, T)
            pe.wait_ge(ffn_in, 16 * N_FFN)
            for c in range(KC):
                ins = pe.matmul(bank[4][0:B, 0:E], zsum[:, c, :], gw_sb[:, c, :], start=(c == 0), stop=(c == KC - 1))
            ins.then_inc(gate_pe, 1)
            pe.wait_ge(gate_dve, 13)
            for k in range(TOPK):
                ins = pe.transpose(bank[5][0:E, k * B:(k + 1) * B], pick[:, k, :], ident[0:B, 0:B])
            ins.then_inc(gate_pe, 1)
            pe.matmul(bank[4][:, 0:T * TOPK], const[0:B, C_SPREAD:C_SPREAD + P], ctile[:].rearrange("p t k -> p (t k)"),
                      start=True, stop=True).then_inc(gate_pe, 1)
            pe.wait_ge(gate_dve, 14)
            for a in range(2):
                ins = pe.matmul(bank[6][0:FH, a * TOPK * B:(a + 1) * TOPK * B], b1_sb[:, a * FH:(a + 1) * FH],
                                pickT[:].rearrange("e k b -> e (k b)"), start=True, stop=True)
            ins.then_inc(gate_pe, 1)
            pe.wait_ge(irow_in, 16)
            pe.wait_ge(gate_dve, 16)

            expert = [[[pe.alloc_register(f"expert{i}_{b}_{k}") for k in range(TOPK)] for b in range(BT)] for i in range(2)]

            def number(i, b, k):
                return pe.snap(expert[i][b][k], min_val=0, max_val=E - 1)

            def expert_step(j, i, load, up, down):
                if up:
                    t = j - 1
                    pe.wait_ge(hs_ready, t + 1)
                    reached(pe, hb_ready, t)
                    for n in range(TOPK * 2):
                        ins = pe.transpose(bank[2][0:FH, n * P:(n + 1) * P], hs[:, n, :], ident)
                    ins.then_inc(ht_done, 1)
                if load:
                    alone(pe, setup_dve)
                    pe.wait_ge(zt_kept, j + 1)
                    reached(pe, hs_ready, j - 1)
                    for k in range(TOPK):
                        for b in range(BT):
                            pe.reg_load(expert[i][b][k], irow[0:1, bass.ds(j * (BT * TOPK) + (b * TOPK + k), 1)])
                            e = number(i, b, k)
                            for c in range(KC):
                                ins = pe.matmul(bank[i][:, k * F:(k + 1) * F], zd[i][:, c, b, :],
                                                w1_sb[:, bass.ds(e, 1), c, :].rearrange("p e f -> p (e f)"),
                                                start=(b + c == 0), stop=(b + c == BT + KC - 2))
                    ins.then_inc(h_done, 1)
                if up:
                    alone(pe, setup_dve)
                    pe.wait_ge(hd_ready, t + 1)
                    reached(pe, res_ready, t - 1)
                    for k in range(TOPK):
                        for b in range(BT):
                            e = number(1 - i, b, k)
                            for a in range(2):
                                rows = FH + 1 if a == 0 else FH
                                ins = pe.matmul(bank[5 - i][:, k * H:(k + 1) * H], hd[0:rows, k * 2 + a, b, :],
                                                w2_sb[0:rows, bass.ds(e, 1), a, :].rearrange("p e h -> p (e h)"),
                                                start=(b + a == 0), stop=(b + a == BT))
                    ins.then_inc(y_done, 1)

            expert_steps(pe, expert_step)


def kernel(x, ctx_2048, mask_BxS2_bk0, L0_attn_Wqkv, L0_attn_bqkv, L0_attn_Wout, L0_attn_bout, L0_xattn_norm_w,
           L0_xattn_wq, L0_xattn_wk, L0_xattn_wv, L0_xattn_wo, L0_xattn_wg, L0_ffn_gate_W, L0_ffn_W1, L0_ffn_b1,
           L0_ffn_W2, L0_ffn_b2):
    import concourse.bacc as _bacc
    from concourse.bass_utils import run_bass_kernel_spmd as _run

    def turned(w):
        return np.ascontiguousarray(np.asarray(w).T)

    def by_heads(w):
        return np.ascontiguousarray(np.asarray(w).T.reshape(HP, 2, HD, H).transpose(0, 2, 1, 3).reshape(P, 2, H))

    bqkv = np.asarray(L0_attn_bqkv)
    arrays = {
        "x": np.ascontiguousarray(np.asarray(x).reshape(B * S, H)),
        "ctxT": turned(np.asarray(ctx_2048).reshape(B * S, H)),
        "hidden": np.ascontiguousarray(np.asarray(mask_BxS2_bk0)).reshape(B * S),
        "consts": shape_constants(),
        "wqkvT": turned(L0_attn_Wqkv),
        "bqk_cols": np.ascontiguousarray(bqkv[0:2 * H].reshape(2 * KC, P).T),
        "bv_cols": np.ascontiguousarray(bqkv[2 * H:].reshape(HP, 2, HD).transpose(0, 2, 1).reshape(P, 2)),
        "woutT": by_heads(L0_attn_Wout),
        "bout": np.ascontiguousarray(L0_attn_bout),
        "nw_cols": np.ascontiguousarray(np.asarray(L0_xattn_norm_w).reshape(KC, P).T),
        "wqT": turned(L0_xattn_wq),
        "wkT": turned(L0_xattn_wk),
        "wvT": turned(L0_xattn_wv),
        "woT": by_heads(L0_xattn_wo),
        "wgT": turned(L0_xattn_wg),
        "gateT": turned(L0_ffn_gate_W),
        "w1": np.ascontiguousarray(L0_ffn_W1),
        "b1": np.ascontiguousarray(L0_ffn_b1),
        "w2": np.ascontiguousarray(L0_ffn_W2),
        "b2": np.ascontiguousarray(L0_ffn_b2),
    }
    nc = _bacc.Bacc("TRN2", target_bir_lowering=False, num_devices=1)
    args = [nc.dram_tensor(n, a.shape, mybir.dt.from_np(a.dtype), kind="ExternalInput").ap() for n, a in arrays.items()]
    out = nc.dram_tensor("out", (B * S, H), F32, kind="ExternalOutput").ap()
    decoder_layer(nc, *args, out)
    r = _run(nc, [arrays], core_ids=[0])
    return np.asarray(r.results[0]["out"]).reshape(B, S, H)
```

```python
from contextlib import ExitStack

import numpy as np

import concourse.bass as bass
from concourse import mybir

ALU = mybir.AluOpType
ACT = mybir.ActivationFunctionType
AX = mybir.AxisListType
F32 = mybir.dt.float32
U32 = mybir.dt.uint32
U8 = mybir.dt.uint8

B, S, H = 32, 64, 256
NH, HD = 16, 16
E, F, TOPK = 6, 176, 2
P = 128
KC = H // P
BT = P // S
T = B // BT
HP = NH // 2
HQ = P // (2 * HD)
FH = F // 2
VW = HD + 1
SELF, CROSS = 0, 1
WARM_START, WARM_CHOICE = 10, 11
HIDDEN = -1e30
FLOOR = -1e29
LN_EPS, RMS_EPS = 1e-5, 1e-6

C_IDENT = 0
C_CAUSAL = C_IDENT + P
C_HEADS = C_CAUSAL + S
C_IOTA = C_HEADS + 2 * S
C_TILE = C_IOTA + E
C_SPREAD = C_TILE + T
C_END = C_SPREAD + P


def shape_constants():
    c = np.zeros((P, C_END), np.float32)
    p = np.arange(P)
    c[:, C_IDENT:C_IDENT + P] = np.eye(P)
    c[:, C_CAUSAL:C_CAUSAL + S] = np.where(np.arange(S)[None] > (p % S)[:, None], HIDDEN, 0.0)
    for odd in range(2):
        c[:, C_HEADS + odd * S:C_HEADS + (odd + 1) * S] = ((p // HD % 2 == odd) * HD ** -0.5)[:, None]
    c[:, C_IOTA:C_IOTA + E] = np.arange(E)
    c[:B, C_TILE:C_TILE + T] = (p[:B, None] // BT == np.arange(T)[None])
    c[:B, C_SPREAD:C_SPREAD + P] = (p[:B, None] % BT == (p // S)[None])
    return c


def decoder_layer(nc, x, ctxT, hidden, consts, wqkvT, bqk_cols, bv_cols, woutT, bout, nw_cols, wqT, wkT, wvT, woT, wgT,
                  gateT, w1, b1, w2, b2, out):
    ctx = ExitStack()
    with ctx:
        def sb(name, shape, dt=F32):
            return ctx.enter_context(nc.sbuf_tensor(name, shape, dt))

        def sem(name):
            return ctx.enter_context(nc.semaphore(name))

        bank = [ctx.enter_context(nc.psum_tensor(f"bank{i}", [P, 512], F32)) for i in range(8)]


        X = sb("X", [P, T, H])
        const = sb("const", [P, C_END])
        ident = const[:, C_IDENT:C_IDENT + P]
        causal = const[:, C_CAUSAL:C_CAUSAL + S]
        heads = const[:, C_HEADS:C_HEADS + 2 * S].rearrange("p (h q) -> p h q", h=2)
        ones = sb("ones", [P, P])
        minus_half = sb("minus_half", [P, 1])
        ln_eps = sb("ln_eps", [P, 1])
        rms_eps = sb("rms_eps", [P, 1])
        mf = [None] + [sb(f"mf{l}", [P, T, 2]) for l in (1, 2)]

        wqkv_sb = sb("wqkv_sb", [P, KC, 3 * H])
        bqk = sb("bqk", [P, 2 * KC])
        bv = sb("bv", [P, 2])
        bout_row = sb("bout_row", [1, H])
        wo_sb = [sb("wout_sb", [P, 2, H]), sb("wo_sb", [P, 2, H])]
        nw = sb("nw", [P, KC])
        wx = {n: sb(f"w{n}_sb", [P, KC, H]) for n in "qkvg"}
        bvb = sb("bvb", [P, 2, P])
        bias_rows = sb("bias_rows", [P, H])
        cT = [sb(f"cT{i}", [P, KC, P]) for i in range(2)]
        hid8 = sb("hid8", [P, B * S], U8)
        hide = sb("hide", [P, B * S])

        six0 = sb("six0", [P, 6])
        mv0 = sb("mv0", [P, 4])
        six1 = sb("six1", [P, 6])
        mv1 = sb("mv1", [P, 4])
        xn = sb("xn", [P, H])
        xnT = sb("xnT", [P, KC, P])
        zn = sb("zn", [P, H])
        qm = sb("qm", [P, KC, BT, 2, S])
        kd = sb("kd", [P, KC, HQ, P])
        vd = [sb(f"vd{i}", [P, NH, BT, VW]) for i in range(2)]
        th = [sb(f"th{i}", [P, H]) for i in range(2)]
        sm = [sb(f"sm{c}", [P, HQ, BT, S]) for c in range(KC)]
        mx = [sb(f"mx{c}", [P, BT * HQ]) for c in range(KC)]
        pr = [sb(f"pr{c}", [P, HQ, BT, S]) for c in range(KC)]
        pT = [sb(f"pT{c}", [P, HQ, P]) for c in range(KC)]
        rsum = sb("rsum", [P, HP, BT])
        rinv = sb("rinv", [P, HP, BT])
        on = sb("on", [P, BT, HP, HD])
        oT = sb("oT", [P, 2, BT, S])
        gated = sb("gated", [P, H])

        w1_sb = sb("w1_sb", [P, E, KC, F])
        w2_sb = sb("w2_sb", [FH + 1, E, 2, H])
        b1_sb = sb("b1_sb", [E, F])
        gw_sb = sb("gw_sb", [P, KC, E])
        zT = sb("zT", [P, KC, B * S])
        zsum = sb("zsum", [P, KC, B])
        zt = [sb(f"zt{i}", [P, KC, P]) for i in range(2)]
        w1c = [sb(f"w1c{i}", [P, BT, TOPK, KC * F]) for i in range(2)]
        w2c = [sb(f"w2c{i}", [FH + 1, BT, TOPK, 2 * H]) for i in range(2)]
        logit = sb("logit", [B, 8])
        top = sb("top", [B, 8])
        ntop = sb("ntop", [B, 1])
        ex = sb("ex", [B, E])
        exs = sb("exs", [B, 2])
        prob = sb("prob", [B, 8])
        p8 = sb("p8", [B, 8])
        i8 = sb("i8", [B, 8], U32)
        i8f = sb("i8f", [B, TOPK])
        cs = sb("cs", [B, 2])
        cw = sb("cw", [B, TOPK])
        pick = sb("pick", [B, TOPK, E])
        pickT = sb("pickT", [E, TOPK, B])
        ctile = sb("ctile", [B, T, TOPK])
        ctok = sb("ctok", [P, T, TOPK])
        irow = sb("irow", [1, B * TOPK], U32)
        b1s = sb("b1s", [FH, B, TOPK, 2])
        hs = sb("hs", [P, TOPK * 2, FH])
        hb = [sb(f"hb{k}", [FH, 2, P]) for k in range(TOPK)]
        hT = [sb(f"hT{k}", [FH + 1, 2, P]) for k in range(TOPK)]
        part = sb("part", [P, H])
        res = [sb(f"res{i}", [P, H]) for i in range(2)]

        x_in0, x_in1, c_in, qkv_in, w_in, cross_in, ffn_in = (
            sem(n) for n in ("x_in0", "x_in1", "c_in", "qkv_in", "w_in", "cross_in", "ffn_in"))
        ctx_in = [sem(f"ctx_in{i}") for i in range(2)]
        setup_pool, setup_dve, setup_act, bias_mm, bias_b, bias_ready = (
            sem(n) for n in ("setup_pool", "setup_dve", "setup_act", "bias_mm", "bias_b", "bias_ready"))
        six0_ready, mv0_ready, factor0 = sem("six0_ready"), sem("mv0_ready"), sem("factor0")
        six1_ready, mv1_ready = sem("six1_ready"), sem("mv1_ready")
        factor1 = [sem(f"factor1_{l}") for l in range(2)]
        mf_ready = [None] + [sem(f"mf_ready{l}") for l in (1, 2)]
        xn_ready, xb_ready = sem("xn_ready"), sem("xb_ready")
        x_done, xT_ready = sem("x_done"), sem("xT_ready")
        q_done, k_done, v_done, g_done = (sem(n) for n in ("q_done", "k_done", "v_done", "g_done"))
        q_ready, v_ready, th_ready = (
            sem(n) for n in ("q_ready", "v_ready", "th_ready"))
        kd_ready = [sem(f"kd_ready{c}") for c in range(KC)]
        s_done = [sem(f"s_done{c}") for c in range(KC)]
        masked = [sem(f"masked{c}") for c in range(KC)]
        mx_ready = [sem(f"mx_ready{c}") for c in range(KC)]
        mx_kept = [sem(f"mx_kept{c}") for c in range(KC)]
        less = [sem(f"less{c}") for c in range(KC)]
        pr_ready = [sem(f"pr_ready{c}") for c in range(KC)]
        t_done = [sem(f"t_done{c}") for c in range(KC)]
        pT_ready = [sem(f"pT_ready{c}") for c in range(KC)]
        pv_done, sum_kept, sum_inv, on_ready = (sem(n) for n in ("pv_done", "sum_kept", "sum_inv", "on_ready"))
        o_done, oT_ready, wo_done, gate_done, x_ready = (
            sem(n) for n in ("o_done", "oT_ready", "wo_done", "gate_done", "x_ready"))
        z_ready, zt_done, zT_ready, zs_ready = (sem(n) for n in ("z_ready", "zt_done", "zT_ready", "zs_ready"))
        gate_dve, gate_pe, gate_act, index_ready, irow_in = (
            sem(n) for n in ("gate_dve", "gate_pe", "gate_act", "index_ready", "irow_in"))
        w1_first, w1_start, w1_second, w2_dve = (sem(n) for n in ("w1_first", "w1_start", "w1_second", "w2_dve"))
        w2_in = [sem(f"w2_in{i}") for i in range(2)]
        ht_done = [sem(f"ht_done{k}") for k in range(TOPK)]
        hb_ready = [sem(f"hb_ready{k}") for k in range(TOPK)]
        hT_ready = [sem(f"hT_ready{k}") for k in range(TOPK)]
        zt_kept, h_done, hs_ready, y_done, part_ready, res_ready = (
            sem(n) for n in ("zt_kept", "h_done", "hs_ready", "y_done", "part_ready", "res_ready"))
        stored = [sem(f"stored{i}") for i in range(2)]

        N_C, N_W, N_CROSS, N_FFN = 2, 6, 4, 6

        def reached(eng, s, n):
            if not isinstance(n, int) or n > 0:
                eng.wait_ge(s, n)

        def alone(eng, s):
            eng.wait_ge(s, 1)

        def held(eng, n):
            return n if isinstance(n, int) else eng.snap(eng.to_reg(n))

        def tile_of(buf, t):
            return buf[:, bass.ds(t, 1), :].rearrange("p a h -> p (a h)")

        def attention_steps(eng, step):
            step(-1, 1, SELF, None, None, None)
            step(0, 0, SELF, SELF, None, None)
            step(1, 1, SELF, SELF, SELF, None)
            step(2, 0, SELF, SELF, SELF, SELF)
            with eng.Fori(3, T - 2, 2) as j:
                step(j, 1, SELF, SELF, SELF, SELF)
                step(j + 1, 0, SELF, SELF, SELF, SELF)
            step(T - 1, 1, CROSS, SELF, SELF, SELF)
            step(T, 0, CROSS, CROSS, SELF, SELF)
            step(T + 1, 1, CROSS, CROSS, CROSS, SELF)
            step(T + 2, 0, CROSS, CROSS, CROSS, CROSS)
            step(T + 3, 1, CROSS, CROSS, CROSS, CROSS)
            step(T + 4, 0, CROSS, CROSS, CROSS, CROSS)
            with eng.Fori(T + 5, 2 * T - 2, 2) as j:
                step(j, 1, CROSS, CROSS, CROSS, CROSS)
                step(j + 1, 0, CROSS, CROSS, CROSS, CROSS)
            step(2 * T - 1, 1, None, CROSS, CROSS, CROSS)
            step(2 * T, 0, None, None, CROSS, CROSS)
            step(2 * T + 1, 1, None, None, None, CROSS)
            step(2 * T + 2, 0, None, None, None, None)
            step(2 * T + 3, 1, None, None, None, None)

        def z_tile(j, lc, behind):
            if not isinstance(j, int):
                return j - behind - T if lc == CROSS else None
            return j - behind - T if 0 <= j - behind - T < T else None

        def expert_steps(eng, step):
            step(-1, 1, True, False, False, False)
            step(0, 0, True, True, False, False)
            step(1, 1, True, True, True, False)
            step(2, 0, True, True, True, True)
            step(3, 1, True, True, True, True)
            with eng.Fori(4, T - 3, 2) as j:
                step(j, 0, True, True, True, True)
                step(j + 1, 1, True, True, True, True)
            step(T - 2, 0, True, True, True, True)
            step(T - 1, 1, False, True, True, True)
            step(T, 0, False, False, True, True)
            step(T + 1, 1, False, False, False, True)

        def expert_of(eng, t, b, k):
            return eng.value_load(irow[0:1, bass.ds(t * (BT * TOPK) + (b * TOPK + k), 1)], min_val=0, max_val=E - 1)

        def w1_of(e):
            return w1_sb[:, bass.ds(e, 1), :, :].rearrange("p e c f -> p (e c f)")

        def w2_of(e):
            return w2_sb[:, bass.ds(e, 1), :, :].rearrange("p e a h -> p (e a h)")

        block = ctx.enter_context(nc.Block())

        @block.sync
        def _(sp):
            xt = x.rearrange("(t p) h -> p t h", p=P)
            sp.dma_start(X[:, 0:2, :], xt[:, 0:2, :]).then_inc(x_in0, 16)
            sp.dma_start(wqkv_sb[:], wqkvT.rearrange("(c p) o -> p c o", p=P)).then_inc(qkv_in, 16)
            sp.dma_start(X[:, 2:T, :], xt[:, 2:T, :]).then_inc(x_in1, 16)
            sp.dma_start(wo_sb[SELF][:], woutT).then_inc(w_in, 16)
            sp.dma_start(wx["q"][:], wqT.rearrange("(c p) o -> p c o", p=P)).then_inc(w_in, 16)
            sp.dma_start(wx["g"][:], wgT.rearrange("(c p) o -> p c o", p=P)).then_inc(w_in, 16)
            sp.dma_start(bv[:], bv_cols).then_inc(w_in, 16)
            sp.dma_start(nw[:], nw_cols).then_inc(w_in, 16)
            sp.dma_start(bout_row[:], bout.rearrange("(a h) -> a h", a=1)).then_inc(w_in, 16)
            sp.dma_start(hid8[:], hidden.rearrange("(a n) -> a n", a=1).to_broadcast([P, B * S])).then_inc(cross_in, 16)
            sp.dma_start(wx["k"][:], wkT.rearrange("(c p) o -> p c o", p=P)).then_inc(cross_in, 16)
            sp.dma_start(wx["v"][:], wvT.rearrange("(c p) o -> p c o", p=P)).then_inc(cross_in, 16)
            sp.dma_start(wo_sb[CROSS][:], woT).then_inc(cross_in, 16)

            def step(j, i, ln, la, lb, lc):
                if la == CROSS:
                    if not isinstance(j, int) or j > T + 1:
                        sp.wait_ge(v_done, j - 1)
                    sp.dma_start(cT[i][:], ctxT.rearrange("(c p) n -> p c n", p=P)[:, :, bass.ds((j - T) * P, P)]
                                 ).then_inc(ctx_in[i], 16)
                if isinstance(j, int) and j == T:
                    sp.dma_start(w1_sb[:], w1.rearrange("e (c p) f -> p e c f", p=P)).then_inc(ffn_in, 16)
                    sp.dma_start(w2_sb[0:FH, :, :, :], w2.rearrange("e (a p) h -> p e a h", p=FH)).then_inc(ffn_in, 16)
                    for a in range(2):
                        sp.dma_start(w2_sb[FH:FH + 1, :, a, :], b2.rearrange("(q e) h -> q e h", q=1)).then_inc(ffn_in, 16)
                    sp.dma_start(b1_sb[:], b1).then_inc(ffn_in, 16)
                    sp.dma_start(gw_sb[:], gateT.rearrange("(c p) e -> p c e", p=P)).then_inc(ffn_in, 16)

            attention_steps(sp, step)

            sp.wait_ge(index_ready, 1)
            sp.dma_start(irow[:], i8[:, 0:TOPK]).then_inc(irow_in, 16)

            sp.wait_ge(irow_in, 16)
            sp.wait_ge(ffn_in, 16 * N_FFN)

            def expert_step(j, i, ahead, load, up, down):
                if load:
                    reached(sp, y_done, j - 1)
                    for k in range(TOPK):
                        sp.dma_start(w2c[i][:, 1, k, :], w2_of(expert_of(sp, j, 1, k))).then_inc(w2_in[i], 16)
                if down:
                    sp.wait_ge(res_ready, j - 1)
                    sp.dma_start(out[bass.ds((j - 2) * P, P), :], res[i][:]).then_inc(stored[i], 16)

            expert_steps(sp, expert_step)
            for i in range(2):
                sp.wait_ge(stored[i], 16 * (T // 2))

        @block.gpsimd
        def _(pool):
            pool.memset(minus_half[:], -0.5).then_inc(setup_pool, 1)
            pool.memset(ln_eps[:], LN_EPS).then_inc(setup_pool, 1)
            pool.memset(rms_eps[:], RMS_EPS).then_inc(setup_pool, 1)
            pool.memset(kd[:], 0.0).then_inc(setup_pool, 1)
            for i in range(2):
                pool.memset(vd[i][:], 0.0).then_inc(setup_pool, 1)
            pool.wait_ge(setup_pool, 6)
            for i in range(2):
                for b in range(BT):
                    pool.memset(vd[i][b * S:(b + 1) * S, :, b, HD:VW], 1.0).then_inc(setup_pool, 1)
            pool.wait_ge(setup_pool, 10)

            def step(j, i, ln, la, lb, lc):
                def entering_factor():
                    n = j + 1
                    pool.wait_ge(mv0_ready, n + 1)
                    pool.tensor_tensor(mv0[:, 3:4], mv0[:, 1:2], ln_eps[:], ALU.add).then_inc(factor0, 1)
                    pool.wait_ge(factor0, 2 * n + 1)
                    pool.tensor_tensor(mv0[:, 2:3], mv0[:, 3:4], minus_half[:], ALU.pow).then_inc(factor0, 1)

                def less_max(c):
                    t = j - 1
                    maxima = held(pool, t + 1)
                    if lb == CROSS:
                        alone(pool, setup_pool)
                    pool.wait_ge(mx_ready[c], maxima)
                    if lb == CROSS:
                        pool.tensor_scalar(mx[c][:], mx[c][:], FLOOR, None, ALU.max).then_inc(mx_kept[c], 1)
                        pool.wait_ge(mx_kept[c], t - T + 1)
                    s3 = sm[c][:].rearrange("p h b k -> p (h b) k")
                    pool.tensor_tensor(s3, s3, mx[c][:].unsqueeze(2).to_broadcast([P, BT * HQ, S]), ALU.subtract
                                       ).then_inc(less[c], 1)

                if lb is not None:
                    for c in range(KC):
                        less_max(c)
                if ln == SELF:
                    entering_factor()
                if lb == SELF:
                    t = j - 1
                    alone(pool, setup_pool)
                    if isinstance(j, int) and j == 1:
                        pool.wait_ge(bias_ready, 1)
                    pool.wait_ge(xn_ready, t + 1)
                    pool.tensor_tensor(tile_of(X, t), tile_of(X, t), bias_rows[:], ALU.add).then_inc(xb_ready, 1)
                if lc is not None:
                    t = j - 2
                    u = t - lc * T
                    chain, a, r, f = factor1[lc], mv1[:, 3:4], mv1[:, 1:2], mv1[:, 2:3]
                    per = 7 if lc == SELF else 2
                    pool.wait_ge(mv1_ready, t + 1)
                    pool.tensor_tensor(a, r, ln_eps[:], ALU.add).then_inc(chain, 1)
                    pool.wait_ge(chain, per * u + 1)
                    pool.tensor_tensor(f, a, minus_half[:], ALU.pow).then_inc(chain, 1)
                    if lc == SELF:
                        pool.wait_ge(chain, per * u + 2)
                        pool.tensor_tensor(a, r, f, ALU.mult).then_inc(chain, 1)
                        pool.wait_ge(chain, per * u + 3)
                        pool.tensor_tensor(a, a, f, ALU.mult).then_inc(chain, 1)
                        pool.wait_ge(chain, per * u + 4)
                        pool.tensor_tensor(a, a, rms_eps[:], ALU.add).then_inc(chain, 1)
                        pool.wait_ge(chain, per * u + 5)
                        pool.tensor_tensor(a, a, minus_half[:], ALU.pow).then_inc(chain, 1)
                        pool.wait_ge(chain, per * u + 6)
                        pool.tensor_tensor(f, f, a, ALU.mult).then_inc(chain, 1)
                    alone(pool, setup_pool)
                    pool.wait_ge(chain, per * u + per)
                    pool.tensor_copy(tile_of(mf[lc + 1], u), mv1[:, 0:3:2]).then_inc(mf_ready[lc + 1], 1)

            attention_steps(pool, step)

            def expert_step(j, i, ahead, load, up, down):
                if ahead:
                    n = j + 1
                    alone(pool, setup_pool)
                    reached(pool, h_done, j)
                    first = isinstance(j, int) and j == -1
                    if first:
                        pool.wait_ge(zT_ready, T)
                    pool.tensor_copy(zt[1 - i][:], zT[:, :, bass.ds(n * P, P)]).then_inc(zt_kept, 1)
                    if first:
                        pool.wait_ge(irow_in, 16)
                        pool.wait_ge(ffn_in, 16 * N_FFN)
                    else:
                        for k in range(TOPK):
                            ins = pool.tensor_copy(w1c[1 - i][:, 1, k, :], w1_of(expert_of(pool, n, 1, k)))
                        ins.then_inc(w1_second, 1)

            expert_steps(pool, expert_step)

        @block.scalar
        def _(act):
            act.dma_start(const[:], consts).then_inc(c_in, 16)
            act.dma_start(bqk[:], bqk_cols).then_inc(c_in, 16)
            act.wait_ge(setup_pool, 1)
            act.activation(mx[0][:, 0:1], minus_half[:], ACT.Exp).then_inc(setup_act, 1)

            def step(j, i, ln, la, lb, lc):
                if isinstance(j, int) and j == 0:
                    act.wait_ge(c_in, 16 * N_C)
                    act.wait_ge(setup_pool, 10)
                if isinstance(j, int) and j == 2:
                    act.wait_ge(bias_mm, 1)
                    act.copy(bias_rows[:], bank[3][:, 0:H]).then_inc(bias_ready, 1)
                if lc is not None:
                    t = j - 2
                    for c in range(KC):
                        act.wait_ge(t_done[c], t + 1)
                        reached(act, pv_done, t)
                        act.copy(pT[c][:].rearrange("p h q -> p (h q)"), bank[c][:]).then_inc(pT_ready[c], 1)

                def keys(layer, t, c):
                    if c == 0:
                        act.wait_ge(k_done, t + 1)
                        act.wait_ge(v_done, t + 1)
                    reached(act, s_done[c], t)
                    for r in range(HQ):
                        rows = slice(r * 2 * HD, (r + 1) * 2 * HD)
                        k = bank[7][rows, c * P:(c + 1) * P]
                        if layer == SELF:
                            ins = act.activation(kd[rows, c, r, :], k, ACT.Identity, bias=bqk[rows, KC + c:KC + c + 1])
                        else:
                            ins = act.copy(kd[rows, c, r, :], k)
                    ins.then_inc(kd_ready[c], 1)

                if lb is not None:
                    keys(lb, j - 1, 1)
                if la is not None:
                    act.wait_ge(x_done, j + 1)
                    reached(act, v_done, j)
                    if la == CROSS:
                        reached(act, g_done, j - T)
                    if z_tile(j, lc, 4) is not None:
                        act.wait_ge(zt_done, z_tile(j, lc, 4) + 1)
                    act.copy(xnT[:].rearrange("p c t -> p (c t)"), bank[2][:, 0:H]).then_inc(xT_ready, 1)
                tz = z_tile(j, lc, 4)
                if tz is not None:
                    alone(act, setup_dve)
                    act.wait_ge(zt_done, tz + 1)
                    act.copy(zT[:, :, bass.ds(tz * P, P)], bank[2][:, H:2 * H].rearrange("p (c t) -> p c t", c=KC)
                             ).then_inc(zT_ready, 1)

                def softmax(c):
                    t = j - 1
                    act.wait_ge(less[c], t + 1)
                    reached(act, t_done[c], t)
                    act.activation(pr[c][:].rearrange("p h b k -> p (h b k)"), sm[c][:].rearrange("p h b k -> p (h b k)"),
                                   ACT.Exp).then_inc(pr_ready[c], 1)

                if lb is not None:
                    softmax(0)
                if lc is not None:
                    t = j - 2
                    act.wait_ge(o_done, t + 1)
                    reached(act, wo_done, t)
                    act.copy(oT[:].rearrange("p h b q -> p b h q"), bank[2][:, 0:H].rearrange("p (b h q) -> p b h q", b=BT, h=2)
                             ).then_inc(oT_ready, 1)
                if la is not None:
                    keys(la, j, 0)
                if lb is not None:
                    softmax(1)
                if la is not None:
                    reached(act, pv_done, j - 1)
                    for b in range(BT):
                        rows = slice(b * S, (b + 1) * S)
                        ins = act.copy(vd[i][rows, :, b, 0:HD], bank[7][rows, H:2 * H].rearrange("p (h d) -> p h d", d=HD))
                    ins.then_inc(v_ready, 1)
                if la == CROSS:
                    act.wait_ge(g_done, j - T + 1)
                    reached(act, gate_done, j - T - 1)
                    act.activation(th[i][:], bank[6][:, H:2 * H], ACT.Tanh, scale=0.5).then_inc(th_ready, 1)

            attention_steps(act, step)

            act.wait_ge(gate_dve, 3)
            act.activation(ex[:], logit[:, 0:E], ACT.Exp, bias=ntop[:, 0:1], accum_out=exs[:, 0:1]).then_inc(gate_act, 1)

            act.wait_ge(irow_in, 16)
            act.wait_ge(ffn_in, 16 * N_FFN)

            def expert_step(j, i, ahead, load, up, down):
                if up:
                    t = j - 1
                    for k in range(TOPK):
                        act.wait_ge(hb_ready[k], t + 1)
                        reached(act, y_done, t)
                        act.activation(hT[k][0:FH, :, :].rearrange("p a t -> p (a t)"), hb[k][:].rearrange("p a t -> p (a t)"),
                                       ACT.Gelu).then_inc(hT_ready[k], 1)
                if load:
                    act.wait_ge(h_done, j + 1)
                    for k in range(TOPK):
                        reached(act, ht_done[k], j)
                    act.copy(hs[:].rearrange("p n f -> p (n f)"), bank[i][:, 0:TOPK * F]).then_inc(hs_ready, 1)
                if ahead:
                    alone(act, setup_dve)
                    reached(act, h_done, j)
                    for k in range(TOPK):
                        ins = act.copy(w1c[1 - i][:, 0, k, :], w1_of(expert_of(act, j + 1, 0, k)))
                    ins.then_inc(w1_first, 1)

            expert_steps(act, expert_step)

        @block.vector
        def _(dve):
            dve.memset(ones[:], 1.0).then_inc(setup_dve, 1)
            for k in range(TOPK):
                dve.memset(hT[k][:], 1.0).then_inc(setup_dve, 1)
            dve.memset(logit[:], HIDDEN).then_inc(setup_dve, 1)
            dve.memset(prob[:], -1.0).then_inc(setup_dve, 1)
            dve.wait_ge(setup_dve, 5)

            def fold():
                dve.wait_ge(w_in, 16 * N_W)
                for h in range(2):
                    ins = dve.tensor_scalar(bvb[:, h, :], ones[:], bv[:, h:h + 1], None, ALU.mult)
                ins.then_inc(bias_b, 1)
                for n in "qg":
                    for c in range(KC):
                        ins = dve.tensor_scalar(wx[n][:, c, :], wx[n][:, c, :], nw[:, c:c + 1], None, ALU.mult)
                ins.then_inc(bias_b, 1)

            def step(j, i, ln, la, lb, lc):
                if isinstance(j, int) and j == 1:
                    fold()
                def entering_stats():
                    n = j + 1
                    alone(dve, setup_dve)
                    if isinstance(j, int) and j < 2:
                        dve.wait_ge(*((x_in1, 16) if n > 1 else (x_in0, 16)))
                    reached(dve, mv0_ready, n)
                    dve.bn_stats(six0[:], tile_of(X, n)).then_inc(six0_ready, 1)

                def entering_mean():
                    n = j + 1
                    n1 = held(dve, n + 1)
                    alone(dve, setup_dve)
                    dve.wait_ge(six0_ready, n1)
                    reached(dve, xn_ready, n)
                    dve.bn_aggr(mv0[:, 0:2], six0[:]).then_inc(mv0_ready, 1)

                if isinstance(j, int) and j == T:
                    dve.wait_ge(cross_in, 16 * N_CROSS)
                    dve.tensor_scalar(hide[:], hid8[:], -1.0, -HIDDEN, ALU.add, ALU.mult).then_inc(setup_dve, 1)
                    dve.wait_ge(setup_dve, 6)
                def mask_and_max(c):
                    t = j - 1
                    scores = bank[4 + c][:].rearrange("p (b h k) -> p b h k", b=BT, h=HQ)
                    dve.wait_ge(s_done[c], t + 1)
                    reached(dve, pr_ready[c], t)
                    if lb == SELF:
                        m = causal.unsqueeze(1).to_broadcast([P, BT, S])
                    else:
                        m = hide[:, bass.ds((t - T) * P, P)].rearrange("p (b k) -> p b k", b=BT)
                    dve.tensor_tensor(sm[c][:].rearrange("p h b k -> p b h k"), scores,
                                      m.unsqueeze(2).to_broadcast([P, BT, HQ, S]), ALU.add).then_inc(masked[c], 1)
                    dve.wait_ge(masked[c], t + 1)
                    dve.tensor_reduce(mx[c][:], sm[c][:].rearrange("p h b k -> p (h b) k"), AX.X, ALU.max
                                      ).then_inc(mx_ready[c], 1)
                if lb is not None:
                    mask_and_max(0)
                if lc is not None:
                    t = j - 2
                    O = bank[3][:, 0:HP * BT * VW].rearrange("p (h b d) -> p h b d", h=HP, b=BT)
                    dve.wait_ge(pv_done, t + 1)
                    reached(dve, on_ready, t)
                    if lc == SELF:
                        dve.tensor_scalar(rsum[:], O[:, :, :, HD], 1.0, None, ALU.mult).then_inc(sum_kept, 1)
                    else:
                        dve.tensor_scalar(rsum[:], O[:, :, :, HD], 1e-30, 2.0, ALU.max, ALU.mult).then_inc(sum_kept, 1)
                    dve.wait_ge(sum_kept, t + 1)
                    dve.reciprocal(rinv[:], rsum[:]).then_inc(sum_inv, 1)
                    dve.wait_ge(sum_inv, t + 1)
                    reached(dve, o_done, t)
                    dve.tensor_tensor(on[:].rearrange("p b h d -> p h b d"), O[:, :, :, 0:HD],
                                      rinv[:].unsqueeze(3).to_broadcast([P, HP, BT, HD]), ALU.mult).then_inc(on_ready, 1)
                def queries():
                    if isinstance(j, int) and j == 0:
                        dve.wait_ge(c_in, 16 * N_C)
                    dve.wait_ge(q_done, j + 1)
                    reached(dve, s_done[1], j)
                    if la == SELF:
                        for c in range(KC):
                            for b in range(BT):
                                qc = bank[6][:, c * P + b * S:c * P + (b + 1) * S].unsqueeze(1).to_broadcast([P, 2, S])
                                ins = dve.scalar_tensor_tensor(out=qm[:, c, b, :, :], in0=qc, scalar=bqk[:, c:c + 1],
                                                               in1=heads, op0=ALU.add, op1=ALU.mult)
                    else:
                        qc = bank[6][:, 0:H].rearrange("p (n q) -> p n q", q=S)
                        ins = dve.tensor_tensor(qm[:].rearrange("p c b h q -> p (c b) h q"),
                                                qc.unsqueeze(2).to_broadcast([P, KC * BT, 2, S]),
                                                heads.unsqueeze(1).to_broadcast([P, KC * BT, 2, S]), ALU.mult)
                    ins.then_inc(q_ready, 1)

                if ln == SELF:
                    entering_stats()
                if lb is not None:
                    mask_and_max(1)
                if ln == SELF:
                    entering_mean()
                def normed():
                    n = j + 1
                    reached(dve, x_done, n)
                    if ln == SELF:
                        dve.wait_ge(factor0, 2 * n + 2)
                        mean, factor = mv0[:, 0:1], mv0[:, 2:3]
                    else:
                        dve.wait_ge(mf_ready[1], n - T + 1)
                        mean, factor = tile_of(mf[1], n - T)[:, 0:1], tile_of(mf[1], n - T)[:, 1:2]
                    dve.tensor_scalar(xn[:], tile_of(X, n - ln * T), mean, factor, ALU.subtract, ALU.mult).then_inc(xn_ready, 1)

                first = isinstance(j, int) and j == 0
                if first:
                    normed()
                if la is not None:
                    queries()
                if ln is not None and not first:
                    normed()
                tz = z_tile(j, lc, 3)
                if tz is not None:
                    m = tile_of(mf[2], tz)
                    dve.wait_ge(mf_ready[2], tz + 1)
                    reached(dve, zt_done, tz)
                    dve.tensor_scalar(zn[:], tile_of(X, tz), m[:, 0:1], m[:, 1:2], ALU.subtract, ALU.mult).then_inc(z_ready, 1)
                tz = z_tile(j, lc, 4)
                if tz is not None:
                    alone(dve, setup_dve)
                    dve.wait_ge(zT_ready, tz + 1)
                    zt = zT[:, :, bass.ds(tz * P, P)].rearrange("p c (b s) -> p c b s", b=BT)
                    dve.tensor_reduce(zsum[:, :, bass.ds(tz * BT, BT)], zt, AX.X, ALU.add).then_inc(zs_ready, 1)
                if lc is not None:
                    t = j - 2
                    xt = tile_of(X, t - lc * T)
                    wo = bank[3][:, 0:H]
                    dve.wait_ge(wo_done, t + 1)
                    if lc == SELF:
                        dve.wait_ge(xb_ready, t + 1)
                        dve.tensor_tensor(xt, wo, xt, ALU.add).then_inc(x_ready, 1)
                    else:
                        dve.wait_ge(th_ready, t - T + 1)
                        dve.scalar_tensor_tensor(out=gated[:], in0=th[i][:], scalar=1.0, in1=wo, op0=ALU.add, op1=ALU.mult
                                                 ).then_inc(gate_done, 1)
                        dve.wait_ge(gate_done, t - T + 1)
                        dve.tensor_tensor(xt, gated[:], xt, ALU.add).then_inc(x_ready, 1)
                    alone(dve, setup_dve)
                    dve.wait_ge(x_ready, t + 1)
                    dve.bn_stats(six1[:], xt).then_inc(six1_ready, 1)
                    if lc == SELF:
                        alone(dve, setup_dve)
                        reached(dve, mf_ready[1], t)
                    else:
                        dve.wait_ge(mf_ready[1], T)
                        reached(dve, mf_ready[2], t - T)
                    dve.wait_ge(six1_ready, t + 1)
                    dve.bn_aggr(mv1[:, 0:2], six1[:]).then_inc(mv1_ready, 1)

            attention_steps(dve, step)

            dve.wait_ge(gate_pe, 1)
            dve.tensor_scalar(logit[:, 0:E], bank[4][0:B, 0:E], 1.0 / S, None, ALU.mult).then_inc(gate_dve, 1)
            dve.wait_ge(gate_dve, 1)
            dve.max(top[:], logit[:]).then_inc(gate_dve, 1)
            dve.wait_ge(gate_dve, 2)
            dve.max_index(i8[:], top[:], logit[:]).then_inc(index_ready, 1)
            dve.tensor_scalar(ntop[:], top[:, 0:1], -1.0, None, ALU.mult).then_inc(gate_dve, 1)
            dve.wait_ge(gate_act, 1)
            dve.reciprocal(exs[:, 1:2], exs[:, 0:1]).then_inc(gate_dve, 1)
            dve.wait_ge(gate_dve, 4)
            dve.tensor_scalar(prob[:, 0:E], ex[:], exs[:, 1:2], None, ALU.mult).then_inc(gate_dve, 1)
            dve.wait_ge(gate_dve, 5)
            dve.max(p8[:], prob[:]).then_inc(gate_dve, 1)
            dve.wait_ge(gate_dve, 6)
            dve.tensor_tensor(cs[:, 0:1], p8[:, 0:1], p8[:, 1:2], ALU.add).then_inc(gate_dve, 1)
            dve.wait_ge(gate_dve, 7)
            dve.reciprocal(cs[:, 1:2], cs[:, 0:1]).then_inc(gate_dve, 1)
            dve.wait_ge(index_ready, 1)
            dve.tensor_copy(i8f[:], i8[:, 0:TOPK]).then_inc(gate_dve, 1)
            dve.wait_ge(gate_dve, 9)
            dve.tensor_scalar(cw[:], p8[:, 0:TOPK], cs[:, 1:2], None, ALU.mult).then_inc(gate_dve, 1)
            for k in range(TOPK):
                ins = dve.tensor_scalar(pick[:, k, :], const[0:B, C_IOTA:C_IOTA + E], i8f[:, k:k + 1], None, ALU.is_equal)
            ins.then_inc(gate_dve, 1)
            dve.wait_ge(gate_dve, 11)
            dve.tensor_tensor(ctile[:], const[0:B, C_TILE:C_TILE + T].unsqueeze(2).to_broadcast([B, T, TOPK]),
                              cw[:].unsqueeze(1).to_broadcast([B, T, TOPK]), ALU.mult).then_inc(gate_dve, 1)
            def keep_spread():
                dve.wait_ge(gate_pe, 2)
                dve.tensor_copy(pickT[:].rearrange("e k b -> e (k b)"), bank[5][0:E, 0:TOPK * B]).then_inc(gate_dve, 1)
                dve.wait_ge(gate_pe, 3)
                dve.tensor_copy(ctok[:].rearrange("p t k -> p (t k)"), bank[4][:, 0:T * TOPK]).then_inc(gate_dve, 1)
                dve.wait_ge(gate_pe, 4)
                dve.tensor_copy(b1s[:].rearrange("p b k a -> p a k b"),
                                bank[6][0:FH, 0:2 * TOPK * B].rearrange("p (a k b) -> p a k b", a=2, k=TOPK)).then_inc(gate_dve, 1)
                dve.wait_ge(gate_dve, 15)

            dve.wait_ge(irow_in, 16)
            dve.wait_ge(ffn_in, 16 * N_FFN)

            for k in range(TOPK):
                ins = dve.tensor_copy(w1c[0][:, 1, k, :], w1_of(expert_of(dve, 0, 1, k)))
            ins.then_inc(w1_start, 1)

            def expert_step(j, i, ahead, load, up, down):
                if up:
                    t = j - 1
                    for k in range(TOPK):
                        bias = b1s[:, bass.ds(t * BT, BT), k, :].rearrange("p b a -> p a b")
                        dve.wait_ge(ht_done[k], t + 1)
                        reached(dve, hT_ready[k], t)
                        dve.tensor_tensor(hb[k][:].rearrange("p a (b t) -> p a b t", b=BT),
                                          bank[2 + k][0:FH, 0:2 * P].rearrange("p (a b t) -> p a b t", b=BT, t=S),
                                          bias.unsqueeze(3).to_broadcast([FH, 2, BT, S]), ALU.add).then_inc(hb_ready[k], 1)
                if down:
                    t = j - 2
                    ct = tile_of(ctok, t)
                    dve.wait_ge(y_done, t + 1)
                    reached(dve, res_ready, t)
                    y = bank[4 + i]
                    dve.scalar_tensor_tensor(out=part[:], in0=y[:, 0:H], scalar=ct[:, 0:1], in1=tile_of(X, t),
                                             op0=ALU.mult, op1=ALU.add).then_inc(part_ready, 1)
                    dve.wait_ge(part_ready, t + 1)
                    if not isinstance(j, int) or j > 3:
                        dve.wait_ge(stored[i], 8 * (t - i))
                    dve.scalar_tensor_tensor(out=res[i][:], in0=y[:, H:2 * H], scalar=ct[:, 1:2], in1=part[:],
                                             op0=ALU.mult, op1=ALU.add).then_inc(res_ready, 1)
                if load:
                    alone(dve, setup_dve)
                    reached(dve, y_done, j - 1)
                    for k in range(TOPK):
                        ins = dve.tensor_copy(w2c[i][:, 0, k, :], w2_of(expert_of(dve, j, 0, k)))
                    ins.then_inc(w2_dve, 1)
                if isinstance(j, int) and j == 0:
                    keep_spread()

            expert_steps(dve, expert_step)

        @block.tensor
        def _(pe):
            def constant_output():
                pe.wait_ge(w_in, 16 * N_W)
                pe.wait_ge(bias_b, 2)
                pe.matmul(bank[3][:, 0:H], ones[0:1, :], bout_row[:], start=True, stop=False)
                for h in range(2):
                    ins = pe.matmul(bank[3][:, 0:H], bvb[:, h, :], wo_sb[SELF][:, h, :], start=False, stop=(h == 1))
                ins.then_inc(bias_mm, 1)

            def keep_busy(n):
                for _ in range(n):
                    pe.matmul(bank[7][:, 0:P], ones[:], ones[:], start=True, stop=True)

            pe.wait_ge(setup_dve, 1)
            keep_busy(WARM_START)
            pe.wait_ge(c_in, 16 * N_C)

            def step(j, i, ln, la, lb, lc):
                if lc is not None:
                    t = j - 2
                    for c in range(KC):
                        pe.wait_ge(pr_ready[c], t + 1)
                        reached(pe, pT_ready[c], t)
                        for r in range(HQ):
                            ins = pe.transpose(bank[c][:, r * P:(r + 1) * P], pr[c][:, r, :, :].rearrange("p b k -> p (b k)"), ident)
                        ins.then_inc(t_done[c], 1)
                if la is not None:
                    pe.wait_ge(xn_ready, j + 1)
                    reached(pe, oT_ready, j - 2)
                    for c in range(KC):
                        ins = pe.transpose(bank[2][:, c * P:(c + 1) * P], xn[:, c * P:(c + 1) * P], ident)
                    ins.then_inc(x_done, 1)
                if isinstance(j, int) and j == 0:
                    keep_busy(2)
                tz = z_tile(j, lc, 4)
                if tz is not None:
                    pe.wait_ge(z_ready, tz + 1)
                    reached(pe, zT_ready, tz)
                    for c in range(KC):
                        ins = pe.transpose(bank[2][:, H + c * P:H + (c + 1) * P], zn[:, c * P:(c + 1) * P], ident)
                    ins.then_inc(zt_done, 1)

                def scores(c):
                    t = j - 1
                    if c == 0:
                        pe.wait_ge(q_ready, t + 1)
                    pe.wait_ge(kd_ready[c], t + 1)
                    reached(pe, masked[c], t)
                    for b in range(BT):
                        ins = pe.matmul(bank[4 + c][:, b * HQ * S:(b + 1) * HQ * S], qm[:, c, b, :, :].rearrange("p h q -> p (h q)"),
                                        kd[:, c, :, b * S:(b + 1) * S], start=True, stop=True)
                    ins.then_inc(s_done[c], 1)

                if lb is not None:
                    scores(0)
                if lc is not None:
                    t = j - 2
                    pe.wait_ge(v_ready, t + 1)
                    if isinstance(j, int) and j == 2:
                        pe.wait_ge(bias_ready, 1)
                    reached(pe, x_ready, t)
                    for c in range(KC):
                        pe.wait_ge(pT_ready[c], t + 1)
                        for r in range(HQ):
                            for h in range(2):
                                hp = c * HQ + r
                                ins = pe.matmul(bank[3][h * S:(h + 1) * S, hp * BT * VW:(hp + 1) * BT * VW],
                                                pT[c][:, r, h * S:(h + 1) * S],
                                                vd[i][:, 2 * hp + h, :, :].rearrange("p b d -> p (b d)"), start=True, stop=True)
                    ins.then_inc(pv_done, 1)
                if lb is not None:
                    scores(1)
                def outputs_transposed():
                    t = j - 2
                    pe.wait_ge(on_ready, t + 1)
                    if la is not None:
                        pe.wait_ge(xT_ready, j + 1)
                    if tz is not None:
                        pe.wait_ge(zT_ready, tz + 1)
                    for b in range(BT):
                        ins = pe.transpose(bank[2][:, b * P:(b + 1) * P], on[:, b, :, :].rearrange("p h d -> p (h d)"), ident)
                    ins.then_inc(o_done, 1)

                def queries():
                    reached(pe, q_ready, j)
                    if la == CROSS:
                        reached(pe, th_ready, j - T)
                    for o in range(KC):
                        for c in range(KC):
                            ins = pe.matmul(bank[6][:, o * P:(o + 1) * P], wq[:, c, o * P:(o + 1) * P], xnT[:, c, :],
                                            start=(c == 0), stop=(c == KC - 1))
                    ins.then_inc(q_done, 1)

                if la is not None:
                    if isinstance(j, int) and j == 0:
                        pe.wait_ge(qkv_in, 16)
                    if isinstance(j, int) and j == T:
                        pe.wait_ge(cross_in, 16 * N_CROSS)
                    wq, wk = (wqkv_sb[:, :, 0:H], wqkv_sb[:, :, H:2 * H]) if la == SELF else (wx["q"][:], wx["k"][:])
                    wv = wqkv_sb[:, :, 2 * H:3 * H] if la == SELF else wx["v"][:]
                    source = xnT[:] if la == SELF else cT[i][:]
                    pe.wait_ge(xT_ready, j + 1)
                    if la == CROSS:
                        pe.wait_ge(ctx_in[i], 8 * (j - (T + i)) + 16)
                    reached(pe, kd_ready[1], j)
                    reached(pe, v_ready, j)
                    for o in range(KC):
                        for c in range(KC):
                            ins = pe.matmul(bank[7][:, o * P:(o + 1) * P], wk[:, c, o * P:(o + 1) * P], source[:, c, :],
                                            start=(c == 0), stop=(c == KC - 1))
                    ins.then_inc(k_done, 1)
                    if la == CROSS:
                        queries()
                        if lc is not None:
                            outputs_transposed()
                    for c in range(KC):
                        ins = pe.matmul(bank[7][:, H:2 * H], source[:, c, :], wv[:, c, :], start=(c == 0), stop=(c == KC - 1))
                    ins.then_inc(v_done, 1)
                if lc is not None and la != CROSS:
                    outputs_transposed()
                if la == SELF:
                    queries()
                if lc is not None:
                    pe.wait_ge(oT_ready, t + 1)
                    for h in range(2):
                        ins = pe.matmul(bank[3][:, 0:H], oT[:, h, :, :].rearrange("p b q -> p (b q)"), wo_sb[lc][:, h, :],
                                        start=(h == 0), stop=(h == 1))
                    ins.then_inc(wo_done, 1)
                if la == CROSS:
                    pe.wait_ge(q_ready, j + 1)
                    for c in range(KC):
                        ins = pe.matmul(bank[6][:, H:2 * H], xnT[:, c, :], wx["g"][:, c, :], start=(c == 0), stop=(c == KC - 1))
                    ins.then_inc(g_done, 1)
                if isinstance(j, int) and j == 1:
                    constant_output()

            attention_steps(pe, step)

            def spread():
                pe.wait_ge(gate_dve, 12)
                for k in range(TOPK):
                    ins = pe.transpose(bank[5][0:E, k * B:(k + 1) * B], pick[:, k, :], ident[0:B, 0:B])
                ins.then_inc(gate_pe, 1)
                pe.matmul(bank[4][:, 0:T * TOPK], const[0:B, C_SPREAD:C_SPREAD + P], ctile[:].rearrange("p t k -> p (t k)"),
                          start=True, stop=True).then_inc(gate_pe, 1)
                pe.wait_ge(gate_dve, 13)
                for a in range(2):
                    ins = pe.matmul(bank[6][0:FH, a * TOPK * B:(a + 1) * TOPK * B], b1_sb[:, a * FH:(a + 1) * FH],
                                    pickT[:].rearrange("e k b -> e (k b)"), start=True, stop=True)
                ins.then_inc(gate_pe, 1)

            pe.wait_ge(zs_ready, T)
            pe.wait_ge(ffn_in, 16 * N_FFN)
            for c in range(KC):
                ins = pe.matmul(bank[4][0:B, 0:E], zsum[:, c, :], gw_sb[:, c, :], start=(c == 0), stop=(c == KC - 1))
            ins.then_inc(gate_pe, 1)
            keep_busy(WARM_CHOICE)

            def expert_step(j, i, ahead, load, up, down):
                if up:
                    t = j - 1
                    pe.wait_ge(hs_ready, t + 1)
                    for k in range(TOPK):
                        reached(pe, hb_ready[k], t)
                        for a in range(2):
                            ins = pe.transpose(bank[2 + k][0:FH, a * P:(a + 1) * P], hs[:, k * 2 + a, :], ident)
                        ins.then_inc(ht_done[k], 1)
                if load:
                    pe.wait_ge(zt_kept, j + 1)
                    pe.wait_ge(w1_first, j + 1)
                    if isinstance(j, int) and j == 0:
                        pe.wait_ge(w1_start, 1)
                    else:
                        pe.wait_ge(w1_second, j)
                    reached(pe, hs_ready, j - 1)
                    for k in range(TOPK):
                        for c in range(KC):
                            for b in range(BT):
                                ins = pe.matmul(bank[i][b * S:(b + 1) * S, k * F:(k + 1) * F], zt[i][:, c, b * S:(b + 1) * S],
                                                w1c[i][:, b, k, c * F:(c + 1) * F], start=(c == 0), stop=(c == KC - 1))
                    ins.then_inc(h_done, 1)
                if isinstance(j, int) and j == 0:
                    spread()
                if up:
                    if isinstance(j, int) and j == 1:
                        pe.wait_ge(gate_dve, 15)
                    pe.wait_ge(w2_dve, t + 1)
                    pe.wait_ge(w2_in[1 - i], 8 * TOPK * (t - (1 - i)) + 16 * TOPK)
                    reached(pe, res_ready, t - 1)
                    for k in range(TOPK):
                        pe.wait_ge(hT_ready[k], t + 1)
                        for a in range(2):
                            for b in range(BT):
                                rows = FH + 1 if a == 0 else FH
                                ins = pe.matmul(bank[5 - i][b * S:(b + 1) * S, k * H:(k + 1) * H],
                                                hT[k][0:rows, a, b * S:(b + 1) * S],
                                                w2c[1 - i][0:rows, b, k, a * H:(a + 1) * H], start=(a == 0), stop=(a == 1))
                    ins.then_inc(y_done, 1)

            expert_steps(pe, expert_step)


def kernel(x, ctx_2048, mask_BxS2_bk0, L0_attn_Wqkv, L0_attn_bqkv, L0_attn_Wout, L0_attn_bout, L0_xattn_norm_w,
           L0_xattn_wq, L0_xattn_wk, L0_xattn_wv, L0_xattn_wo, L0_xattn_wg, L0_ffn_gate_W, L0_ffn_W1, L0_ffn_b1,
           L0_ffn_W2, L0_ffn_b2):
    import concourse.bacc as _bacc
    from concourse.bass_utils import run_bass_kernel_spmd as _run

    def turned(w):
        return np.ascontiguousarray(np.asarray(w).T)

    def by_heads(w):
        return np.ascontiguousarray(np.asarray(w).T.reshape(HP, 2, HD, H).transpose(0, 2, 1, 3).reshape(P, 2, H))

    bqkv = np.asarray(L0_attn_bqkv)
    arrays = {
        "x": np.ascontiguousarray(np.asarray(x).reshape(B * S, H)),
        "ctxT": turned(np.asarray(ctx_2048).reshape(B * S, H)),
        "hidden": np.ascontiguousarray(np.asarray(mask_BxS2_bk0)).reshape(B * S),
        "consts": shape_constants(),
        "wqkvT": turned(L0_attn_Wqkv),
        "bqk_cols": np.ascontiguousarray(bqkv[0:2 * H].reshape(2 * KC, P).T),
        "bv_cols": np.ascontiguousarray(bqkv[2 * H:].reshape(HP, 2, HD).transpose(0, 2, 1).reshape(P, 2)),
        "woutT": by_heads(L0_attn_Wout),
        "bout": np.ascontiguousarray(L0_attn_bout),
        "nw_cols": np.ascontiguousarray(np.asarray(L0_xattn_norm_w).reshape(KC, P).T),
        "wqT": turned(L0_xattn_wq),
        "wkT": turned(L0_xattn_wk),
        "wvT": turned(L0_xattn_wv),
        "woT": by_heads(L0_xattn_wo),
        "wgT": turned(L0_xattn_wg),
        "gateT": turned(L0_ffn_gate_W),
        "w1": np.ascontiguousarray(L0_ffn_W1),
        "b1": np.ascontiguousarray(L0_ffn_b1),
        "w2": np.ascontiguousarray(L0_ffn_W2),
        "b2": np.ascontiguousarray(L0_ffn_b2),
    }
    nc = _bacc.Bacc("TRN2", target_bir_lowering=False, num_devices=1)
    args = [nc.dram_tensor(n, a.shape, mybir.dt.from_np(a.dtype), kind="ExternalInput").ap() for n, a in arrays.items()]
    out = nc.dram_tensor("out", (B * S, H), F32, kind="ExternalOutput").ap()
    decoder_layer(nc, *args, out)
    r = _run(nc, [arrays], core_ids=[0])
    return np.asarray(r.results[0]["out"]).reshape(B, S, H)
```
